# Optimizing a Trainium2 kernel written in Bass

```python
import numpy as np
import jax
import jax.numpy as jnp

def _softmax(x, axis=-1):
    return jax.nn.softmax(x, axis=axis)

def _gelu(x):
    return jax.nn.gelu(x, approximate=True)

def _silu(x):
    return jax.nn.silu(x)

def _sigmoid(x):
    return jax.nn.sigmoid(x)

def _layernorm(x, axis=-1, eps=1e-05):
    m = jnp.mean(x, axis=axis, keepdims=True)
    v = jnp.var(x, axis=axis, keepdims=True)
    return (x - m) / jnp.sqrt(v + eps)

def _scatter_add(tgt, idx, src, axis=0):
    return tgt.at[idx].add(src)

def _segment_sum(src, seg, n):
    return jax.ops.segment_sum(src, seg, n)
kernel_name = 'mk_prb_d1_jaxref_r4_a7467f'

def setup_inputs(seed: int=0):
    np.random.seed(seed)
    _w = jnp.asarray

    def _L0_attn_setup():
        import jax, jax.numpy as jnp
        import numpy as np
        DIM = 512
        HEADS = 16
        HEAD_DIM = DIM // HEADS
        CHUNK = 128
        B, N = (4, 512)

        def _rmsnorm(x, w, eps):
            return x * jax.lax.rsqrt(jnp.mean(x * x, axis=-1, keepdims=True) + eps) * w

        def _weight_quant(w):
            scale = 1.0 / jnp.clip(jnp.mean(jnp.abs(w)), 1e-05, None)
            q = jnp.clip(jnp.round(w * scale), -1.0, 1.0) / scale
            return w + jax.lax.stop_gradient(q - w)

        def _forward(x, qkv_w, qkv_norm_w, proj_w, proj_norm_w, norm_w, s):
            Bb, Nn, C = x.shape
            H, D, T = (HEADS, HEAD_DIM, CHUNK)
            nc = Nn // T
            eps = jnp.finfo(x.dtype).eps
            scale = D ** (-0.5)
            h = _rmsnorm(x, qkv_norm_w, eps)
            qkv = h @ _weight_quant(qkv_w).T
            qkv = qkv.reshape(Bb, Nn, 3, H, D)
            q, k, v = (qkv[:, :, 0], qkv[:, :, 1], qkv[:, :, 2])

            def chunks(t):
                return t.reshape(Bb, nc, T, H, D).transpose(1, 0, 3, 2, 4)
            qc, kc, vc = (chunks(q), chunks(k), chunks(v))
            tt = jnp.arange(T, dtype=x.dtype)
            lam_t = jnp.exp(-s[:, None] * tt)
            lam_rev = jnp.exp(-s[:, None] * (T - tt))
            diff = tt[:, None] - tt[None, :]
            mask = jnp.where(diff >= 0, jnp.exp(-s[:, None, None] * diff), 0.0)
            lam_T = jnp.exp(-s * T)[:, None, None]

            def step(S, qkv_c):
                qi, ki, vi = qkv_c
                scores = jnp.einsum('bhtd,bhsd,hts->bhts', qi, ki, mask)
                intra = jnp.einsum('bhts,bhsd->bhtd', scores, vi)
                cross = jnp.einsum('bhtd,ht,bhde->bhte', qi, lam_t, S)
                o = scale * (intra + cross)
                kv = jnp.einsum('bhtd,ht,bhte->bhde', ki, lam_rev, vi)
                return (lam_T * S + kv, o)
            S0 = jnp.zeros((Bb, H, D, D), x.dtype)
            _, outs = jax.lax.scan(step, S0, (qc, kc, vc))
            out = outs.transpose(1, 0, 3, 2, 4).reshape(Bb, Nn, C)
            out = _rmsnorm(out, norm_w, 1e-06)
            out = _rmsnorm(out, proj_norm_w, eps) @ _weight_quant(proj_w).T
            return out
        key = jax.random.key(seed)
        ks = jax.random.split(key, 3)
        x = jax.random.normal(ks[0], (B, N, DIM), jnp.float32)
        bound = float(1.0 / np.sqrt(DIM))
        qkv_w = jax.random.uniform(ks[1], (3 * DIM, DIM), jnp.float32, -bound, bound)
        proj_w = jax.random.uniform(ks[2], (DIM, DIM), jnp.float32, -bound, bound)
        return {'x': x, 'qkv_w': qkv_w, 'qkv_norm_w': jnp.ones((DIM,), jnp.float32), 'proj_w': proj_w, 'proj_norm_w': jnp.ones((DIM,), jnp.float32), 'norm_w': jnp.ones((DIM,), jnp.float32), 's': jnp.full((HEADS,), 0.02, jnp.float32)}
    _L0_attn_in = _L0_attn_setup()

    def _L0_ffn_setup():
        import jax, jax.numpy as jnp
        import numpy as np
        DIM_IN = 512
        DIM_HIDDEN = 2048
        key = jax.random.key(seed)
        k_x, k_g, k_u, k_d = jax.random.split(key, 4)
        s_in = 1.0 / np.sqrt(DIM_IN)
        s_hid = 1.0 / np.sqrt(DIM_HIDDEN)
        x = jax.random.normal(k_x, (4, 512, DIM_IN), dtype=jnp.float32)
        w_gate = jax.random.uniform(k_g, (DIM_HIDDEN, DIM_IN), jnp.float32, -s_in, s_in)
        w_up = jax.random.uniform(k_u, (DIM_HIDDEN, DIM_IN), jnp.float32, -s_in, s_in)
        w_down = jax.random.uniform(k_d, (DIM_IN, DIM_HIDDEN), jnp.float32, -s_hid, s_hid)
        return {'x': x, 'w_gate': w_gate, 'w_up': w_up, 'w_down': w_down}
    _L0_ffn_in = _L0_ffn_setup()
    _d = {'L0_attn_x': _L0_attn_in['x'], 'L0_attn_qkv_w': _L0_attn_in['qkv_w'], 'L0_attn_qkv_norm_w': _L0_attn_in['qkv_norm_w'], 'L0_attn_proj_w': _L0_attn_in['proj_w'], 'L0_attn_proj_norm_w': _L0_attn_in['proj_norm_w'], 'L0_attn_norm_w': _L0_attn_in['norm_w'], 'L0_attn_s': _L0_attn_in['s'], 'L0_ffn_w_gate': _L0_ffn_in['w_gate'], 'L0_ffn_w_up': _L0_ffn_in['w_up'], 'L0_ffn_w_down': _L0_ffn_in['w_down']}
    _x0 = _d['L0_attn_x']
    _d['L0_attn_x'] = jax.random.normal(jax.random.fold_in(jax.random.key(seed), 1), (4, 1024, 512), dtype=_x0.dtype)
    del _x0
    return _d

def reference(L0_attn_x, L0_attn_qkv_w, L0_attn_qkv_norm_w, L0_attn_proj_w, L0_attn_proj_norm_w, L0_attn_norm_w, L0_attn_s, L0_ffn_w_gate, L0_ffn_w_up, L0_ffn_w_down):

    def _L0_attn_ref(x, qkv_w, qkv_norm_w, proj_w, proj_norm_w, norm_w, s):
        import jax, jax.numpy as jnp
        import numpy as np
        DIM = 512
        HEADS = 16
        HEAD_DIM = DIM // HEADS
        CHUNK = 128
        B, N = (4, 512)

        def _rmsnorm(x, w, eps):
            return x * jax.lax.rsqrt(jnp.mean(x * x, axis=-1, keepdims=True) + eps) * w

        def _weight_quant(w):
            scale = 1.0 / jnp.clip(jnp.mean(jnp.abs(w)), 1e-05, None)
            q = jnp.clip(jnp.round(w * scale), -1.0, 1.0) / scale
            return w + jax.lax.stop_gradient(q - w)

        def _forward(x, qkv_w, qkv_norm_w, proj_w, proj_norm_w, norm_w, s):
            Bb, Nn, C = x.shape
            H, D, T = (HEADS, HEAD_DIM, CHUNK)
            nc = Nn // T
            eps = jnp.finfo(x.dtype).eps
            scale = D ** (-0.5)
            h = _rmsnorm(x, qkv_norm_w, eps)
            qkv = h @ _weight_quant(qkv_w).T
            qkv = qkv.reshape(Bb, Nn, 3, H, D)
            q, k, v = (qkv[:, :, 0], qkv[:, :, 1], qkv[:, :, 2])

            def chunks(t):
                return t.reshape(Bb, nc, T, H, D).transpose(1, 0, 3, 2, 4)
            qc, kc, vc = (chunks(q), chunks(k), chunks(v))
            tt = jnp.arange(T, dtype=x.dtype)
            lam_t = jnp.exp(-s[:, None] * tt)
            lam_rev = jnp.exp(-s[:, None] * (T - tt))
            diff = tt[:, None] - tt[None, :]
            mask = jnp.where(diff >= 0, jnp.exp(-s[:, None, None] * diff), 0.0)
            lam_T = jnp.exp(-s * T)[:, None, None]

            def step(S, qkv_c):
                qi, ki, vi = qkv_c
                scores = jnp.einsum('bhtd,bhsd,hts->bhts', qi, ki, mask)
                intra = jnp.einsum('bhts,bhsd->bhtd', scores, vi)
                cross = jnp.einsum('bhtd,ht,bhde->bhte', qi, lam_t, S)
                o = scale * (intra + cross)
                kv = jnp.einsum('bhtd,ht,bhte->bhde', ki, lam_rev, vi)
                return (lam_T * S + kv, o)
            S0 = jnp.zeros((Bb, H, D, D), x.dtype)
            _, outs = jax.lax.scan(step, S0, (qc, kc, vc))
            out = outs.transpose(1, 0, 3, 2, 4).reshape(Bb, Nn, C)
            out = _rmsnorm(out, norm_w, 1e-06)
            out = _rmsnorm(out, proj_norm_w, eps) @ _weight_quant(proj_w).T
            return out
        return _forward(x, qkv_w, qkv_norm_w, proj_w, proj_norm_w, norm_w, s)

    def _L0_ffn_ref(x, w_gate, w_up, w_down):
        import jax, jax.numpy as jnp
        import numpy as np
        DIM_IN = 512
        DIM_HIDDEN = 2048
        gate = jnp.einsum('bsd,hd->bsh', x, w_gate)
        up = jnp.einsum('bsd,hd->bsh', x, w_up)
        gated = jax.nn.silu(gate) * up
        return jnp.einsum('bsh,dh->bsd', gated, w_down)
    x = L0_attn_x
    xn = _layernorm(x, axis=-1)
    x = x + _L0_attn_ref(xn, L0_attn_qkv_w, L0_attn_qkv_norm_w, L0_attn_proj_w, L0_attn_proj_norm_w, L0_attn_norm_w, L0_attn_s) + _L0_ffn_ref(xn, L0_ffn_w_gate, L0_ffn_w_up, L0_ffn_w_down)
    return x

_drawn_inputs = setup_inputs


def setup_inputs(seed=0):
    import zlib

    import numpy as np

    out = dict(_drawn_inputs(seed))
    spreads = {'L0_attn_qkv_norm_w': (1.0, 0.2),
     'L0_attn_proj_norm_w': (1.0, 0.2),
     'L0_attn_norm_w': (1.0, 0.2),
     'L0_attn_s': (0.019999999552965164, 0.2)}
    factors = {}
    for name, (base, spread) in spreads.items():
        noise = np.random.default_rng([zlib.crc32(name.encode()), seed]).standard_normal(out[name].shape)
        drawn = base * np.exp(spread * noise) if base else spread * noise
        out[name] = jnp.asarray(drawn.astype(out[name].dtype))
    for name, factor in factors.items():
        out[name] = (out[name] * factor).astype(out[name].dtype)
    return out
```

```python
import numpy as np
import concourse.bass as bass
from concourse import mybir

F32, F16, U32, I32 = mybir.dt.float32, mybir.dt.float16, mybir.dt.uint32, mybir.dt.int32
ALU = mybir.AluOpType
ACT = mybir.ActivationFunctionType
AX = mybir.AxisListType

P = 128
D = 512
KT = D // P
HEADS, HD = 16, 32
HPG = P // HD
GROUPS = HEADS // HPG
BATCH, SEQ = 4, 1024
TOK = BATCH * SEQ
BLK = 512
TPB = BLK // P
BPB = SEQ // BLK
NBLK = TOK // BLK
HALF = 2 * P
HID = 2048
HT = HID // P
NQ = 4
HPQ = HT // NQ
STEPS = 2 * GROUPS

LN_EPS, RMS_EPS, OUT_EPS = 1e-5, float(np.finfo(np.float32).eps), 1e-6
MAGIC = 1.5 * 2.0 ** 23
LEAST = 1e-12
X_SCALE = 2.0 ** 10
H_SCALE = 2.0 ** 9
QKV_SCALE = 2.0 ** -4
SCORE_SCALE = 2.0 ** -20
QL_SCALE = 2.0 ** -24
OUT_UNIT = 2.0 ** 32


class Count:

    def __init__(self, nc, name, per, before=0):
        self.sem, self.per, self.before = nc.alloc_semaphore(name), per, before

    def at(self, blk, k):
        if isinstance(blk, int):
            return self.before + self.per * blk + k
        return blk * self.per + (self.before + k)


def schedule():
    tiles = [[(kind, h) for h in range(HPQ * q, HPQ * (q + 1)) for kind in ("G", "U")] for q in range(NQ)]
    down = [[("D", q, c) for c in range(TPB)] for q in range(NQ)]

    def mix(q):
        return [x for n in range(TPB) for x in (*tiles[q][2 * n:2 * n + 2], down[q - 1][n])]

    fill = iter(tiles[0] + mix(1) + mix(2) + tiles[3] + down[2] + down[3])

    def f(n=1):
        return [next(fill) for _ in range(n)]

    seq = [("V", 0), ("V", 1), ("Q", 0), ("K", 0)]
    for s in range(STEPS):
        after = s == GROUPS
        seq += f() + [("SC", s, 0), ("KT", s)]
        seq += [("NR", 0)] * after + f() + [("ZT", 0)] * after + f()
        seq += [("KV", s), ("O", s, 0)] + [("PJ", 0), ("ZT", 1)] * after + [("SC", s, 1)]
        if s + 1 < STEPS:
            seq += [("Q", s + 1), ("K", s + 1)]
        if s + 1 == STEPS:
            seq += [("ST", 0)]
        seq += f() + [("PJ", 1)] * after + f() + [("O", s, 1)]
        if s + 1 == GROUPS:
            seq += [("V", 2), ("NA", 0), ("V", 3), ("NA", 1)]
    seq += f() + [("TX", 0), ("TX", 1), ("NA", 2)] + f() + [("NA", 3)] + f() + [("TH", 0), ("TH", 1), ("NR", 1)]
    seq += f() + [("ZT", 2), ("ST", 1)] + f() + [("PJ", 2), ("ZT", 3), ("TX", 2), ("TX", 3)]
    seq += f() + [("PJ", 3)] + f() + [("TH", 2), ("TH", 3)] + f()
    assert not list(fill)
    return seq


SEQUENCE = schedule()
FIRST_TILES = [("ST", 0), ("TX", 0), ("TX", 1), ("TH", 0), ("TH", 1),
               ("ST", 1), ("TX", 2), ("TX", 3), ("TH", 2), ("TH", 3)]
Y_ADDS = [it for it in SEQUENCE if it[0] in ("D", "PJ")]
POOLED = [it for it in SEQUENCE if it[0] in ("V", "Q", "K", "KT", "KV", "ZT", "PJ", "TX", "TH", "D")]
N_SHARED = 4
assert len(POOLED) % N_SHARED == 0


def build(nc, x, qkv_t, proj_t, gate_t, up_t, down_t, qn_w, on_w, pn_w, s_row, s_part, out):
    def sb(name, shape, dt):
        return nc.alloc_sbuf_tensor(name, shape, dt)

    wg = [sb(f"wg_{n}", [P, KT, HID], F16) for n in ("hi", "lo")]
    wu = [sb(f"wu_{n}", [P, KT, HID], F16) for n in ("hi", "lo")]
    wd = [sb(f"wd_{n}", [P, HT, D], F16) for n in ("hi", "lo")]
    wq = sb("wq", [P, KT, 3 * D], F16)
    wp = sb("wp", [P, KT, D], F16)
    arena = sb("arena", [P, 8192], F32)
    gated = [[arena[:, 2048 * b + 1024 * n:2048 * b + 1024 * (n + 1)].bitcast(F16)
              .rearrange("p (t n) -> p t n", t=HPQ) for n in range(2)] for b in range(2)]
    y = arena[:, 4096:6144].rearrange("p (c n) -> p c n", c=TPB)
    o = arena[:, 6144:7168].rearrange("p (c n) -> p c n", c=2)
    osq = arena[:, 7168:7680]
    z = [arena[:, 7680 + 256 * n:7936 + 256 * n].bitcast(F16).rearrange("p (k t) -> p k t", k=KT)
         for n in range(2)]
    xt = [sb(f"xt_{n}", [P, KT, BLK], F16) for n in ("hi", "lo")]
    ht = [sb(f"ht_{n}", [P, KT, BLK], F16) for n in ("hi", "lo")]
    xin = sb("xin", [P, 2, D], F32)
    v = [sb(f"v_{n}", [P, 2, D], F16) for n in ("hi", "lo")]
    qb = [sb(f"qb_{n}", [P, 2, HPG, P], F16) for n in ("hi", "lo")]
    kf = [sb(f"kf_{n}", [P, HALF], F16) for n in ("hi", "lo")]
    ql = sb("ql", [P, 2, HALF], F32)
    kl = sb("kl", [P, HALF], F32)
    kt = [sb(f"kt_{n}", [P, HALF], F16) for n in ("hi", "lo")]
    kvm = kl[:, :].rearrange("p (c t) -> p c t", c=2)
    state = sb("state", [P, 2, GROUPS, P], F32)
    state1 = sb("state1", [P, P], F32)
    sm = sb("sm", [P, HPG, P], F32)
    smp = [sb(f"sm_{n}", [P, HPG, P], F16) for n in ("hi", "lo")]
    sg = sb("sg", [P, BLK], F32)
    ramp_diff, ramp, ramp_back = sm[:, 2, :], sm[:, 3, :], sg[:, 0:P]
    mask = sb("mask", [P, HEADS, P], F32)
    lam_q = sb("lam_q", [P, GROUPS, P], F32)
    lam_k = sb("lam_k", [P, GROUPS, P], F32)
    diag = sb("diag", [P, P], F32)
    qn_b = sb("qn_b", [P, D], F32)
    on2_b = sb("on2_b", [P, D], F32)
    op_b = sb("op_b", [P, D], F32)
    ident = sb("ident", [P, P], F32)
    sr = sb("sr", [P, HEADS], F32)
    sp = sb("sp", [P, GROUPS], F32)
    head = sb("head", [P, 5, HEADS], F32)
    part = sb("part", [P, 6, GROUPS], F32)
    pm = sb("pm", [P, 16], F32)
    am = sb("am", [P, 16], F32)
    p2 = sb("p2", [P, 16], F32)
    ip = sb("ip", [P, 16], F32)
    ws = sb("ws", [P, 16], F32)
    sgate = sb("sgate", [P, NQ], F32)
    cu = sb("cu", [P, NQ], F32)
    cd = sb("cd", [P, NQ], F32)
    beta = sb("beta", [P, 16], F32)
    st6 = sb("st6", [P, 2, 6], F32)
    idle = sb("idle", [P, 1], F32)
    mv = sb("mv", [P, 2, 2], F32)
    var_ab = sb("var_ab", [P, 3, 2], F32)
    rs = sb("rs", [P, 2, 2], F32)
    mhalf = sb("mhalf", [P, 4], F32)
    nrm = sb("nrm", [P, 5, 2], F32)

    banks = [nc.alloc_psum_tensor(f"bank{n}", [P, 512], F32) for n in range(8)]
    b_gate, b_up, b_sc, b_o = banks[0], banks[1], banks[2], banks[3]
    shared = banks[4:8]

    def bank_of(it):
        return shared[POOLED.index(it) % N_SHARED]

    C = lambda name, per, before=0: Count(nc, name, per, before)
    pe = {k: C("pe_" + k, n, b) for k, n, b in (
        ("V", 4, 0), ("Q", 8, 0), ("K", 8, 0), ("KT", 8, 0), ("KV", 8, 0), ("SC", 16, 0), ("O", 16, 0),
        ("ZT", 4, 1), ("PJ", 4, 0), ("TX", 4, 4), ("TH", 4, 4), ("G", 16, 0), ("U", 16, 0), ("D", 16, 0))}
    ac = {k: C("act_" + k, n, b) for k, n, b in (
        ("V", 4, 0), ("Q", 8, 0), ("K", 8, 0), ("KT", 8, 0), ("SM", 16, 0), ("SQ", 4, 0), ("Z", 4, 0),
        ("TX", 4, 4), ("TH", 4, 4), ("SILU", 16, 1), ("GH", 16, 0))}
    ve = {k: C("dve_" + k, n, b) for k, n, b in (
        ("V", 4, 0), ("Q", 8, 1), ("K", 8, 1), ("KT", 8, 1), ("KVM", 8, 1), ("S1", 8, 0), ("S2", 8, 0),
        ("SM", 16, 1), ("SL", 16, 0), ("OUT", 8, 1), ("SUM", 4, 1), ("U", 2, 0), ("ZN", 4, 0), ("Z", 4, 1),
        ("Y", 20, 21), ("XN", 4, 4), ("H", 4, 4), ("TX", 4, 4), ("TH", 4, 4), ("VAR", 2, 2),
        ("GT", 16, 1), ("GL", 16, 1), ("CHAIN", 12, 12))}
    po = {k: C("pool_" + k, n, b) for k, n, b in (("RS", 2, 2), ("R", 2, 0))}
    ld_x = [C(f"ld_x{n}", 32, 32) for n in range(2)]
    ld_y, st_y = C("ld_y", 16), C("st_y", 64, 16)

    def sem(name):
        return nc.alloc_semaphore(name)

    ld_tab, ld_proj, ld_rows = sem("ld_tab"), sem("ld_proj"), sem("ld_rows")
    ld_qkv = [sem(f"ld_qkv{n}") for n in range(KT)]
    ld_piece = [sem(f"ld_piece{n}") for n in range(3)]
    s_ident, s_iota, s_set, s_exp, s_mask, s_tab = (sem(n) for n in (
        "ident", "iota", "set", "exp", "masked", "tables"))
    s_pro, s_sum, s_tern, s_red, s_all, s_scale, s_whi, s_wlo, s_ones, s_ffn = (sem(n) for n in (
        "pro_chain", "beta_sum", "ternary", "piece_max", "piece_allmax", "piece_scale", "piece_hi",
        "piece_lo", "beta_total", "ffn_ready"))

    pieces = [(kind, q) for q in range(NQ) for kind in ("gate", "up", "down")]
    dram = {"gate": gate_t, "up": up_t, "down": down_t}

    def slot(n):
        return arena[:, 2048 * (n % 3):2048 * (n % 3 + 1)].rearrange("p (k n) -> p k n", k=4)

    def piece_parts(n):
        kind, q = pieces[n]
        if kind == "down":
            return [w[:, HPQ * q:HPQ * (q + 1), :] for w in wd]
        return [w[:, :, 512 * q:512 * (q + 1)] for w in (wg if kind == "gate" else wu)]

    def shared_free(it, blk, executed):
        order = [i for i in POOLED if i in executed]
        n, at = order.index(it), bank_of(it)
        for back in range(1, len(order) + 1):
            other = order[n - back]
            if bank_of(other) is at:
                wrapped = n - back < 0
                break
        if wrapped and isinstance(blk, int):
            return None
        cnt, k = {"D": lambda: (ve["Y"], Y_ADDS.index(other) + 1), "PJ": lambda: (ve["Y"], Y_ADDS.index(other) + 1),
                  "ZT": lambda: (ve["Z"], other[1] + 1), "KV": lambda: (ve["KVM"], other[1] + 1),
                  }.get(other[0], lambda: (ve[other[0]], other[1] + 1))()
        return cnt.sem, cnt.at(blk, k - (cnt.per if wrapped else 0))

    def tensor_item(e, it, blk, executed):
        kind = it[0]
        if kind in ("NA", "NR", "ST"):
            return
        if kind in ("V", "Q", "K", "KT", "KV", "ZT", "PJ", "TX", "TH", "D"):
            free = shared_free(it, blk, executed)
            if free:
                e.wait_ge(*free)
            bank = bank_of(it)

        def products(dst, lhs, rhs, start=True, stop=True):
            for n, (a, b) in enumerate(zip(lhs, rhs)):
                last = e.matmul(dst, a, b, start=start and n == 0, stop=stop and n == len(lhs) - 1)
            return last

        if kind == "V":
            c = it[1]
            e.wait_ge(ve["TH"].sem, ve["TH"].at(blk, c + 1 - 4))
            t = slice(P * c, P * (c + 1))
            products(bank[:, :], [ht[n][:, k, t] for k in range(KT) for n in range(2)],
                     [wq[:, k, 2 * D:3 * D] for k in range(KT) for n in range(2)]).then_inc(pe["V"].sem, 1)
        elif kind in ("Q", "K"):
            s = it[1]
            a, j = divmod(s, GROUPS)
            e.wait_ge(ve["TH"].sem, ve["TH"].at(blk, 2 * a + 2 - 4))
            f = (D if kind == "K" else 0) + P * j
            products(bank[:, 0:HALF], [wq[:, k, f:f + P] for k in range(KT) for n in range(2)],
                     [ht[n][:, k, HALF * a:HALF * (a + 1)] for k in range(KT) for n in range(2)])\
                .then_inc(pe[kind].sem, 1)
        elif kind == "KT":
            s = it[1]
            e.wait_ge(ve["K"].sem, ve["K"].at(blk, s + 1))
            for c in range(2):
                last = e.transpose(bank[:, P * c:P * (c + 1)], kl[:, P * c:P * (c + 1)], ident[:, :])
            last.then_inc(pe["KT"].sem, 1)
        elif kind == "SC":
            _, s, c = it
            e.wait_ge(ve["K"].sem, ve["K"].at(blk, s + 1))
            e.wait_ge(ve["SM"].sem, ve["SM"].at(blk, 2 * s + c))
            t = slice(P * c, P * (c + 1))
            products(b_sc[:, :], [kf[0][:, t], kf[0][:, t], kf[1][:, t]],
                     [qb[n][:, c, :, :] for n in (0, 1, 0)]).then_inc(pe["SC"].sem, 1)
        elif kind == "KV":
            s = it[1]
            j = s % GROUPS
            e.wait_ge(ve["KT"].sem, ve["KT"].at(blk, s + 1))
            e.wait_ge(ve["V"].sem, ve["V"].at(blk, 2 * (s // GROUPS) + 2))
            for c in range(2):
                t, f = slice(P * c, P * (c + 1)), slice(P * j, P * (j + 1))
                last = products(bank[:, t], [kt[0][:, t], kt[0][:, t], kt[1][:, t]],
                                [v[n][:, c, f] for n in (0, 1, 0)])
            last.then_inc(pe["KV"].sem, 1)
        elif kind == "O":
            _, s, c = it
            a, j = divmod(s, GROUPS)
            e.wait_ge(ve["SL"].sem, ve["SL"].at(blk, 2 * s + c + 1))
            if c == 0:
                e.wait_ge(ve["OUT"].sem, ve["OUT"].at(blk, s))
                cross = state[:, a, j, :]
            else:
                e.wait_ge(ve["S1"].sem, ve["S1"].at(blk, s + 1))
                cross = state1[:, :]
            products(b_o[:, P * c:P * (c + 1)], [ql[:, s % 2, P * c:P * (c + 1)]], [cross], stop=False)
            for h in range(HPG):
                f = slice(P * j + HD * h, P * j + HD * (h + 1))
                last = products(b_o[:, P * c + HD * h:P * c + HD * (h + 1)],
                                [smp[0][:, h, :], smp[0][:, h, :], smp[1][:, h, :]],
                                [v[n][:, c, f] for n in (0, 1, 0)], start=False, stop=h == HPG - 1)
            last.then_inc(pe["O"].sem, 1)
        elif kind == "ZT":
            c = it[1]
            e.wait_ge(ve["ZN"].sem, ve["ZN"].at(blk, c + 1))
            for k in range(KT):
                last = e.transpose(bank[:, P * k:P * (k + 1)], o[:, c % 2, P * k:P * (k + 1)], ident[:, :])
            last.then_inc(pe["ZT"].sem, 1)
        elif kind == "PJ":
            c = it[1]
            e.wait_ge(ve["Z"].sem, ve["Z"].at(blk, c + 1))
            products(bank[:, :], [z[n][:, k, :] for k in range(KT) for n in range(2)],
                     [wp[:, k, :] for k in range(KT) for n in range(2)]).then_inc(pe["PJ"].sem, 1)
        elif kind in ("TX", "TH"):
            c = it[1]
            made = ve["XN" if kind == "TX" else "H"]
            e.wait_ge(made.sem, made.at(blk, c + 1))
            for k in range(KT):
                last = e.transpose(bank[:, P * k:P * (k + 1)], xin[:, c % 2, P * k:P * (k + 1)], ident[:, :])
            last.then_inc(pe[kind].sem, 1)
        elif kind in ("G", "U"):
            h = it[1]
            if (kind, h) == ("G", 0):
                e.wait_ge(ve["TX"].sem, ve["TX"].at(blk, 0))
                e.wait_ge(s_ffn, NQ)
            t = slice(P * h, P * (h + 1))
            w, bank, free = (wg, b_gate, ac["SILU"]) if kind == "G" else (wu, b_up, ve["GT"])
            e.wait_ge(free.sem, free.at(blk, h))
            products(bank[:, :], [w[n][:, k, t] for k in range(KT) for n in (0, 0, 1)],
                     [xt[n][:, k, :] for k in range(KT) for n in (0, 1, 0)]).then_inc(pe[kind].sem, 1)
        elif kind == "D":
            _, q, c = it
            e.wait_ge(ve["GL"].sem, ve["GL"].at(blk, HPQ * (q + 1)))
            g, t = gated[q % 2], slice(P * c, P * (c + 1))
            products(bank[:, :], [g[n][:, i, t] for i in range(HPQ) for n in (0, 0, 1)],
                     [wd[n][:, HPQ * q + i, :] for i in range(HPQ) for n in (0, 1, 0)]).then_inc(pe["D"].sem, 1)

    def scalar_item(e, it, blk):
        kind = it[0]
        if kind == "V":
            e.wait_ge(pe["V"].sem, pe["V"].at(blk, it[1] + 1))
            e.activation(v[0][:, it[1] % 2, :], bank_of(it)[:, :], ACT.Copy, scale=QKV_SCALE).then_inc(ac["V"].sem, 1)
        elif kind == "Q":
            e.wait_ge(pe["Q"].sem, pe["Q"].at(blk, it[1] + 1))
            for h in range(HPG):
                r = slice(HD * h, HD * (h + 1))
                last = e.activation(qb[0][r, :, h, :], bank_of(it)[r, 0:HALF].rearrange("p (c t) -> p c t", c=2),
                                    ACT.Copy, scale=QKV_SCALE)
            last.then_inc(ac["Q"].sem, 1)
        elif kind == "K":
            e.wait_ge(pe["K"].sem, pe["K"].at(blk, it[1] + 1))
            e.activation(kf[0][:, :], bank_of(it)[:, 0:HALF], ACT.Copy, scale=QKV_SCALE).then_inc(ac["K"].sem, 1)
        elif kind == "KT":
            e.wait_ge(pe["KT"].sem, pe["KT"].at(blk, it[1] + 1))
            e.activation(kt[0][:, :], bank_of(it)[:, 0:HALF], ACT.Copy).then_inc(ac["KT"].sem, 1)
        elif kind == "SC":
            _, s, c = it
            e.wait_ge(ve["SM"].sem, ve["SM"].at(blk, 2 * s + c + 1))
            e.activation(smp[0][:, :, :], sm[:, :, :], ACT.Copy).then_inc(ac["SM"].sem, 1)
        elif kind == "NA":
            c = it[1]
            e.wait_ge(ve["OUT"].sem, ve["OUT"].at(blk, 4 * (c // 2) + 4))
            e.wait_ge(ve["SUM"].sem, ve["SUM"].at(blk, c))
            e.activation(osq[:, :], o[:, c % 2, :], ACT.Square, accum_out=nrm[:, 0, c % 2:c % 2 + 1])\
                .then_inc(ac["SQ"].sem, 1)
        elif kind == "ZT":
            c = it[1]
            e.wait_ge(pe["ZT"].sem, pe["ZT"].at(blk, c + 1))
            e.activation(z[0][:, :, :], bank_of(it)[:, :].rearrange("p (k t) -> p k t", k=KT), ACT.Copy)\
                .then_inc(ac["Z"].sem, 1)
        elif kind in ("TX", "TH"):
            c = it[1]
            dst, scale = (xt, X_SCALE) if kind == "TX" else (ht, 1.0)
            e.wait_ge(pe[kind].sem, pe[kind].at(blk, c + 1))
            e.activation(dst[0][:, :, P * c:P * (c + 1)], bank_of(it)[:, :].rearrange("p (k t) -> p k t", k=KT),
                         ACT.Copy, scale=scale).then_inc(ac[kind].sem, 1)
        elif kind == "G":
            h = it[1]
            q = h // HPQ
            e.wait_ge(pe["G"].sem, pe["G"].at(blk, h + 1))
            e.wait_ge(ve["GL"].sem, ve["GL"].at(blk, h))
            e.activation(sg[:, :], b_gate[:, :], ACT.Silu, scale=sgate[:, q:q + 1]).then_inc(ac["SILU"].sem, 1)
        elif kind == "U":
            h = it[1]
            q = h // HPQ
            e.wait_ge(ve["GT"].sem, ve["GT"].at(blk, h + 1))
            e.activation(gated[q % 2][0][:, h % HPQ, :], sg[:, :], ACT.Copy).then_inc(ac["GH"].sem, 1)

    chain = [0]

    def vector_item(e, it, blk):
        kind = it[0]

        def lo(dst, src, scale, hi, ready, k):
            e.wait_ge(ready.sem, ready.at(blk, k))
            if scale == 1.0:
                return e.tensor_tensor(dst, src, hi, ALU.subtract)
            return e.scalar_tensor_tensor(out=dst, in0=src, scalar=scale, in1=hi, op0=ALU.mult, op1=ALU.subtract)

        def link(ins):
            chain[0] += 1
            ins.then_inc(ve["CHAIN"].sem, 1)
            e.wait_ge(ve["CHAIN"].sem, ve["CHAIN"].at(blk, chain[0]))

        if kind == "V":
            c = it[1] % 2
            lo(v[1][:, c, :], bank_of(it)[:, :], QKV_SCALE, v[0][:, c, :], ac["V"], it[1] + 1).then_inc(ve["V"].sem, 1)
        elif kind == "Q":
            s = it[1]
            b = bank_of(it)
            for h in range(HPG):
                r = slice(HD * h, HD * (h + 1))
                lo(qb[1][r, :, h, :], b[r, 0:HALF].rearrange("p (c t) -> p c t", c=2), QKV_SCALE,
                   qb[0][r, :, h, :], ac["Q"], s + 1)
            e.tensor_tensor(ql[:, s % 2, :].rearrange("p (c t) -> p c t", c=2),
                            b[:, 0:HALF].rearrange("p (c t) -> p c t", c=2),
                            lam_q[:, s % GROUPS, :].unsqueeze(1).to_broadcast([P, 2, P]), ALU.mult)\
                .then_inc(ve["Q"].sem, 1)
        elif kind == "K":
            s = it[1]
            b = bank_of(it)
            lo(kf[1][:, :], b[:, 0:HALF], QKV_SCALE, kf[0][:, :], ac["K"], s + 1)
            e.tensor_tensor(kl[:, :].rearrange("p (c t) -> p c t", c=2),
                            b[:, 0:HALF].rearrange("p (c t) -> p c t", c=2),
                            lam_k[:, s % GROUPS, :].unsqueeze(1).to_broadcast([P, 2, P]), ALU.mult)\
                .then_inc(ve["K"].sem, 1)
        elif kind == "KT":
            s = it[1]
            lo(kt[1][:, :], bank_of(it)[:, 0:HALF], 1.0, kt[0][:, :], ac["KT"], s + 1).then_inc(ve["KT"].sem, 1)
        elif kind == "SC":
            _, s, c = it
            j, k = s % GROUPS, 2 * s + c + 1
            e.wait_ge(pe["SC"].sem, pe["SC"].at(blk, k))
            e.tensor_tensor(sm[:, :, :], b_sc[:, :].rearrange("p (h t) -> p h t", h=HPG),
                            mask[:, HPG * j:HPG * (j + 1), :], ALU.mult).then_inc(ve["SM"].sem, 1)
            lo(smp[1][:, :, :], sm[:, :, :], 1.0, smp[0][:, :, :], ac["SM"], k).then_inc(ve["SL"].sem, 1)
        elif kind == "KV":
            s = it[1]
            a, j = divmod(s, GROUPS)
            e.wait_ge(pe["KV"].sem, pe["KV"].at(blk, s + 1))
            e.scalar_tensor_tensor(out=kvm, in0=bank_of(it)[:, 0:HALF].rearrange("p (c t) -> p c t", c=2),
                                   scalar=part[:, 5, j:j + 1], in1=diag[:, :].unsqueeze(1).to_broadcast([P, 2, P]),
                                   op0=ALU.mult, op1=ALU.mult).then_inc(ve["KVM"].sem, 1)
            e.wait_ge(ve["KVM"].sem, ve["KVM"].at(blk, s + 1))
            e.scalar_tensor_tensor(out=state1[:, :], in0=state[:, a, j, :], scalar=part[:, 4, j:j + 1],
                                   in1=kvm[:, 0, :], op0=ALU.mult, op1=ALU.add).then_inc(ve["S1"].sem, 1)
            e.wait_ge(ve["S1"].sem, ve["S1"].at(blk, s + 1))
            e.scalar_tensor_tensor(out=state[:, 1 - a, j, :], in0=state1[:, :], scalar=part[:, 4, j:j + 1],
                                   in1=kvm[:, 1, :], op0=ALU.mult, op1=ALU.add).then_inc(ve["S2"].sem, 1)
        elif kind == "O":
            _, s, c = it
            if c == 0:
                return
            a, j = divmod(s, GROUPS)
            e.wait_ge(pe["O"].sem, pe["O"].at(blk, 2 * s + 2))
            e.wait_ge(pe["ZT"].sem, pe["ZT"].at(blk, 2 * a))
            e.tensor_tensor(o[:, :, P * j:P * (j + 1)].rearrange("p c (h d) -> p c h d", h=HPG),
                            b_o[:, 0:HALF].rearrange("p (c h d) -> p c h d", c=2, h=HPG),
                            head[:, 3, HPG * j:HPG * (j + 1)].unsqueeze(1).unsqueeze(3).to_broadcast([P, 2, HPG, HD]),
                            ALU.mult).then_inc(ve["OUT"].sem, 1)
        elif kind == "NA":
            c = it[1]
            e.wait_ge(ac["SQ"].sem, ac["SQ"].at(blk, c + 1))
            e.tensor_tensor_reduce(out=osq[:, :], in0=osq[:, :], in1=on2_b[:, :], scale=1.0, scalar=0.0,
                                   op0=ALU.mult, op1=ALU.add, accum_out=nrm[:, 1, c % 2:c % 2 + 1])\
                .then_inc(ve["SUM"].sem, 1)
        elif kind == "NR":
            a = it[1]
            e.wait_ge(ve["SUM"].sem, ve["SUM"].at(blk, 2 * a + 2))
            link(e.tensor_scalar(nrm[:, 2, :], nrm[:, 0, :], RMS_EPS / D, RMS_EPS * OUT_EPS, ALU.mult, ALU.add))
            e.scalar_tensor_tensor(out=nrm[:, 3, :], in0=nrm[:, 1, :], scalar=1.0 / D, in1=nrm[:, 2, :],
                                   op0=ALU.mult, op1=ALU.add).then_inc(ve["U"].sem, 1)
            e.wait_ge(po["R"].sem, po["R"].at(blk, a + 1))
            for c in range(2):
                e.scalar_tensor_tensor(out=o[:, c, :], in0=o[:, c, :], scalar=nrm[:, 4, c:c + 1], in1=op_b[:, :],
                                       op0=ALU.mult, op1=ALU.mult).then_inc(ve["ZN"].sem, 1)
        elif kind == "ZT":
            c = it[1]
            lo(z[1][:, :, :], bank_of(it)[:, :].rearrange("p (k t) -> p k t", k=KT), 1.0, z[0][:, :, :],
               ac["Z"], c + 1).then_inc(ve["Z"].sem, 1)
        elif kind in ("PJ", "D"):
            c, k = it[-1], Y_ADDS.index(it)
            if all(i[-1] != c for i in Y_ADDS[:k]):
                e.wait_ge(ld_y.sem, ld_y.at(blk, 16))
            mine, n = (pe["PJ"], c + 1) if kind == "PJ" else (pe["D"], TPB * it[1] + c + 1)
            e.wait_ge(mine.sem, mine.at(blk, n))
            e.wait_ge(ve["Y"].sem, ve["Y"].at(blk, k))
            e.scalar_tensor_tensor(out=y[:, c, :], in0=bank_of(it)[:, :],
                                   scalar=beta[:, 8:9] if kind == "PJ" else cd[:, it[1]:it[1] + 1],
                                   in1=y[:, c, :], op0=ALU.mult, op1=ALU.add).then_inc(ve["Y"].sem, 1)
        elif kind == "ST":
            p = it[1]
            for c in range(2):
                e.wait_ge(ld_x[c].sem, ld_x[c].at(blk, 16 * (p + 1)))
                last = e.bn_stats(st6[:, c, :], xin[:, c, :])
            link(last)
            e.memset(idle[:, :], 0.0)
            for c in range(2):
                last = e.bn_aggr(mv[:, c, :], st6[:, c, :])
            link(last)
            link(e.tensor_scalar(var_ab[:, 0, :], mv[:, :, 1], LN_EPS, None, ALU.add))
            link(e.reciprocal(var_ab[:, 2, :], var_ab[:, 0, :]))
            link(e.tensor_tensor(var_ab[:, 2, :], var_ab[:, 2, :], mv[:, :, 1], ALU.mult))
            e.tensor_scalar(var_ab[:, 1, :], var_ab[:, 2, :], RMS_EPS, None, ALU.add).then_inc(ve["VAR"].sem, 1)
            e.wait_ge(po["RS"].sem, po["RS"].at(blk, p + 1))
            for c in range(2):
                e.tensor_scalar(xin[:, c, :], xin[:, c, :], mv[:, c, 0:1], rs[:, 0, c:c + 1],
                                ALU.subtract, ALU.mult).then_inc(ve["XN"].sem, 1)
        elif kind == "TX":
            c = it[1]
            lo(xt[1][:, :, P * c:P * (c + 1)], bank_of(it)[:, :].rearrange("p (k t) -> p k t", k=KT), X_SCALE,
               xt[0][:, :, P * c:P * (c + 1)], ac["TX"], c + 1).then_inc(ve["TX"].sem, 1)
            e.scalar_tensor_tensor(out=xin[:, c % 2, :], in0=xin[:, c % 2, :], scalar=rs[:, 1, c % 2:c % 2 + 1],
                                   in1=qn_b[:, :], op0=ALU.mult, op1=ALU.mult).then_inc(ve["H"].sem, 1)
        elif kind == "TH":
            c = it[1]
            lo(ht[1][:, :, P * c:P * (c + 1)], bank_of(it)[:, :].rearrange("p (k t) -> p k t", k=KT), 1.0,
               ht[0][:, :, P * c:P * (c + 1)], ac["TH"], c + 1).then_inc(ve["TH"].sem, 1)
        elif kind == "U":
            h = it[1]
            q = h // HPQ
            e.wait_ge(pe["U"].sem, pe["U"].at(blk, h + 1))
            e.wait_ge(ac["SILU"].sem, ac["SILU"].at(blk, h + 1))
            e.scalar_tensor_tensor(out=sg[:, :], in0=b_up[:, :], scalar=cu[:, q:q + 1], in1=sg[:, :],
                                   op0=ALU.mult, op1=ALU.mult).then_inc(ve["GT"].sem, 1)
            lo(gated[q % 2][1][:, h % HPQ, :], sg[:, :], 1.0, gated[q % 2][0][:, h % HPQ, :], ac["GH"], h + 1)\
                .then_inc(ve["GL"].sem, 1)

    def pool_item(e, it, blk):
        if it[0] == "ST":
            e.wait_ge(ve["VAR"].sem, ve["VAR"].at(blk, it[1] + 1))
            e.tensor_tensor(rs[:, :, :], var_ab[:, 0:2, :], mhalf[:, :].rearrange("p (a b) -> p a b", a=2), ALU.pow)\
                .then_inc(po["RS"].sem, 1)
        elif it[0] == "NR":
            e.wait_ge(ve["U"].sem, ve["U"].at(blk, it[1] + 1))
            e.tensor_tensor(nrm[:, 4, :], nrm[:, 3, :], mhalf[:, 0:2], ALU.pow).then_inc(po["R"].sem, 1)

    def load_x(e, blk, row, c):
        if not (isinstance(blk, int) and c < 2):
            e.wait_ge(pe["TH"].sem, pe["TH"].at(blk, c - 1))
        src = x[bass.ds(row + P * c, P), :] if not isinstance(row, int) else x[row + P * c:row + P * (c + 1), :]
        e.dma_start(xin[:, c % 2, :], src).then_inc(ld_x[c % 2].sem, 16)

    def blocks(e, body, batch=None):
        with e.Fori(0, BATCH) as b:
            if batch:
                batch()
            with e.Fori(0, BPB) as hb:
                body(b * BPB + hb)

    with nc.Block() as block:
        @block.sync
        def _(e):
            e.sem_inc(st_y.sem, st_y.before)
            for c in range(2):
                load_x(e, -1, 0, c)
            for c in range(KT):
                e.dma_start(arena[:, 1536 * c:1536 * (c + 1)], qkv_t[:, 1536 * c:1536 * (c + 1)]).then_inc(ld_qkv[c], 16)
            e.dma_start(arena[:, 6144:8192], proj_t).then_inc(ld_proj, 16)
            for c in range(2, TPB):
                load_x(e, -1, 0, c)
            for n, (kind, q) in enumerate(pieces):
                if n < 3:
                    e.wait_ge(s_tern, KT)
                else:
                    e.wait_ge(s_wlo, n - 2)
                e.dma_start(slot(n), dram[kind][q, :, :, :]).then_inc(ld_piece[n % 3], 16)
            e.wait_ge(s_wlo, len(pieces))

            def body(blk):
                e.wait_ge(st_y.sem, st_y.at(blk, 0))
                e.dma_start(y[:, :, :], x[bass.ds(blk * BLK, BLK), :].rearrange("(c p) n -> p c n", p=P))\
                    .then_inc(ld_y.sem, 16)
                ahead = (blk + 1) % NBLK * BLK
                for c in range(TPB):
                    load_x(e, blk, ahead, c)
                for c in range(TPB):
                    k = max(n for n, it in enumerate(Y_ADDS) if it[-1] == c) + 1
                    e.wait_ge(ve["Y"].sem, ve["Y"].at(blk, k))
                    e.dma_start(out[bass.ds(blk * BLK + P * c, P), :], y[:, c, :]).then_inc(st_y.sem, 16)

            blocks(e, body)
            e.wait_ge(st_y.sem, st_y.at(NBLK, 0))

        @block.gpsimd
        def _(e):
            e.memset(ident[:, :], 0.0).then_inc(s_ident, 1)
            e.wait_ge(s_ident, 1)
            e.affine_select(out=ident[:, :], in_=ident[:, :], compare_op=ALU.not_equal, fill=1.0, base=0,
                            pattern=[[-1, P]], channel_multiplier=1).then_inc(s_ident, 1)
            e.memset(mhalf[:, :], -0.5).then_inc(s_ident, 1)
            e.iota(sm[:, 0, :].bitcast(I32), [[1, P]], base=0, channel_multiplier=-1).then_inc(s_iota, 1)
            e.iota(sm[:, 1, :].bitcast(I32), [[1, P]], base=0, channel_multiplier=0).then_inc(s_iota, 1)
            e.wait_ge(s_ident, 3)
            for it in FIRST_TILES[:5]:
                pool_item(e, it, -1)
            e.wait_ge(s_exp, 1)
            e.affine_select(out=mask[:, :, :], in_=mask[:, :, :], compare_op=ALU.is_ge, fill=0.0, base=0,
                            pattern=[[0, HEADS], [1, P]], channel_multiplier=-1).then_inc(s_mask, 1)
            for it in FIRST_TILES[5:]:
                pool_item(e, it, -1)
            for n in range(len(pieces)):
                e.wait_ge(s_red, n + 1)
                e.partition_all_reduce(am[:, n:n + 1], pm[:, n:n + 1], P, bass.bass_isa.ReduceOp.max).then_inc(s_all, 1)

            def body(blk):
                for it in SEQUENCE:
                    pool_item(e, it, blk)

            blocks(e, body)

        @block.scalar
        def _(e):
            e.sem_inc(ac["SILU"].sem, ac["SILU"].before)
            for dst, src in ((sr[:, :], s_row.partition_broadcast(P)), (sp[:, :], s_part)):
                e.dma_start(dst, src).then_inc(ld_tab, 16)
            for dst, src in ((qn_b[:, :], qn_w), (on2_b[:, :], on_w), (op_b[:, :], pn_w)):
                e.dma_start(dst, src.partition_broadcast(P)).then_inc(ld_rows, 16)
            e.wait_ge(s_set, 2)
            for h in range(HEADS):
                last = e.activation(mask[:, h, :], ramp_diff, ACT.Exp, scale=head[:, 0, h:h + 1],
                                    bias=head[:, 1, h:h + 1])
            last.then_inc(s_exp, 1)
            for j in range(GROUPS):
                e.activation(lam_q[:, j, :], ramp, ACT.Exp, scale=part[:, 0, j:j + 1], bias=part[:, 1, j:j + 1])
                e.activation(lam_k[:, j, :], ramp_back, ACT.Exp, scale=part[:, 0, j:j + 1], bias=part[:, 2, j:j + 1])
            e.activation(head[:, 2, :], head[:, 1, :], ACT.Exp, scale=-1.0)
            e.activation(part[:, 4, :], part[:, 0, :], ACT.Exp, scale=float(P))
            e.activation(part[:, 5, :], part[:, 2, :], ACT.Exp, scale=-1.0).then_inc(s_exp, 1)
            for it in FIRST_TILES:
                scalar_item(e, it, -1)
            for n in range(len(pieces)):
                e.wait_ge(s_scale, n + 1)
                e.activation(piece_parts(n)[0], slot(n), ACT.Copy, scale=ws[:, n:n + 1]).then_inc(s_whi, 1)

            def body(blk):
                for it in SEQUENCE:
                    scalar_item(e, it, blk)

            blocks(e, body)

        @block.tensor
        def _(e):
            e.sem_inc(pe["ZT"].sem, pe["ZT"].before)
            e.wait_ge(s_ident, 2)
            for it in FIRST_TILES[:5]:
                tensor_item(e, it, -1, FIRST_TILES)
            for n in range(2):
                e.wait_ge(s_sum, n + 1)
                e.matmul(b_gate[:, n:n + 1] if n == 0 else b_up[:, 0:1], state[:, 0, 0, :], beta[:, n:n + 1],
                         start=True, stop=True).then_inc(s_ones, 1)
            for it in FIRST_TILES[5:]:
                tensor_item(e, it, -1, FIRST_TILES)
            e.wait_ge(s_tab, 1)

            def body(blk):
                for it in SEQUENCE:
                    tensor_item(e, it, blk, SEQUENCE)

            blocks(e, body)

        @block.vector
        def _(e):
            done = [0]

            def link(ins):
                done[0] += 1
                ins.then_inc(s_pro, 1)
                e.wait_ge(s_pro, done[0])

            for n in range(2):
                e.memset(qb[n][:, :, :, :].bitcast(U32), 0)
            e.memset(diag[:, :], 0.0)
            link(e.memset(state[:, 0, 0, :], 1.0))
            for h in range(HPG):
                r = slice(HD * h, HD * (h + 1))
                e.memset(diag[r, r], 1.0)
            for name in ("Q", "K", "KT", "KVM", "SM", "OUT", "SUM", "Z", "Y", "GT", "GL"):
                e.sem_inc(ve[name].sem, ve[name].before)
            e.wait_ge(ld_tab, 32)
            e.tensor_scalar(head[:, 0, :], sr[:, :], -1.0, None, ALU.mult)
            e.tensor_scalar(part[:, 0, :], sp[:, :], -1.0, None, ALU.mult)
            e.tensor_scalar(head[:, 1, :], sr[:, :], 0.0, float(P - 1), ALU.min, ALU.mult)
            e.tensor_scalar(part[:, 1, :], sp[:, :], 0.0, float(P - 1), ALU.min, ALU.mult)
            e.tensor_scalar(part[:, 2, :], sp[:, :], 0.0, float(P), ALU.min, ALU.mult).then_inc(s_set, 1)
            e.wait_ge(s_iota, 2)
            e.tensor_scalar(ramp_diff, sm[:, 0, :].bitcast(I32), 0.0, None, ALU.max)
            e.tensor_scalar(ramp_back, sm[:, 1, :].bitcast(I32), -1.0, float(P), ALU.mult, ALU.add)
            e.tensor_copy(ramp, sm[:, 1, :].bitcast(I32)).then_inc(s_set, 1)
            e.wait_ge(ld_rows, 48)
            e.tensor_reduce(am[:, 12:13], qn_b[:, :], axis=AX.X, op=ALU.max, apply_absolute_value=True)
            link(e.tensor_reduce(am[:, 13:14], op_b[:, :], axis=AX.X, op=ALU.max, apply_absolute_value=True))

            def power(a, b):
                link(e.tensor_scalar(am[:, a:b], am[:, a:b], LEAST, None, ALU.max))
                link(e.tensor_scalar(p2[:, a:b].bitcast(U32), am[:, a:b].bitcast(U32), 0x7F800000, None, ALU.bitwise_and))
                link(e.reciprocal(ip[:, a:b], p2[:, a:b]))

            power(12, 14)
            link(e.tensor_scalar(qn_b[:, :], qn_b[:, :], ip[:, 12:13], H_SCALE, ALU.mult, ALU.mult))
            for it in FIRST_TILES[:5]:
                vector_item(e, it, -1)
            link(e.tensor_tensor(op_b[:, :], op_b[:, :], on2_b[:, :], ALU.mult))
            e.tensor_scalar(op_b[:, :], op_b[:, :], ip[:, 13:14], H_SCALE, ALU.mult, ALU.mult)
            e.tensor_tensor(on2_b[:, :], on2_b[:, :], on2_b[:, :], ALU.mult)
            for c in range(KT):
                e.wait_ge(ld_qkv[c], 16)
                last = e.tensor_reduce(beta[:, 12 + c:13 + c], arena[:, 1536 * c:1536 * (c + 1)], axis=AX.X,
                                       op=ALU.add, apply_absolute_value=True)
            link(last)
            e.tensor_reduce(beta[:, 0:1], beta[:, 12:16], axis=AX.X, op=ALU.add).then_inc(s_sum, 1)
            e.wait_ge(ld_proj, 16)
            e.tensor_reduce(beta[:, 1:2], arena[:, 6144:8192], axis=AX.X, op=ALU.add,
                            apply_absolute_value=True).then_inc(s_sum, 1)
            e.wait_ge(s_ones, 2)
            link(e.tensor_scalar(beta[:, 2:3], b_gate[:, 0:1], 1.0 / (3 * D * D), 1e-5, ALU.mult, ALU.max))
            link(e.tensor_scalar(beta[:, 3:4], b_up[:, 0:1], 1.0 / (D * D), 1e-5, ALU.mult, ALU.max))
            link(e.reciprocal(beta[:, 4:6], beta[:, 2:4]))
            for a in range(KT + 1):
                lo_, hi_ = (1536 * a, 1536 * (a + 1)) if a < KT else (6144, 8192)
                w, sc = arena[:, lo_:hi_], beta[:, 4:5] if a < KT else beta[:, 5:6]
                dst = wq[:, a, :] if a < KT else wp[:, :, :].rearrange("p k n -> p (k n)")
                link(e.tensor_scalar(w, w, sc, MAGIC, ALU.mult, ALU.add))
                link(e.tensor_scalar(w, w, -MAGIC, 1.0, ALU.add, ALU.min))
                e.tensor_scalar(dst, w, -1.0, None, ALU.max).then_inc(s_tern, 1)
            link(e.tensor_scalar(beta[:, 6:7], beta[:, 2:3], p2[:, 12:13], 1.0 / H_SCALE, ALU.mult, ALU.mult))
            e.tensor_scalar(beta[:, 8:9], beta[:, 3:4], p2[:, 13:14], 1.0 / H_SCALE, ALU.mult, ALU.mult)
            link(e.tensor_scalar(beta[:, 7:8], beta[:, 6:7], beta[:, 6:7], OUT_UNIT * HD ** -0.5, ALU.mult, ALU.mult))
            e.wait_ge(s_exp, 2)
            link(e.tensor_scalar(head[:, 3, :], head[:, 2, :], beta[:, 6:7], beta[:, 7:8], ALU.mult, ALU.mult))
            e.tensor_scalar(lam_q[:, :, :], lam_q[:, :, :], QL_SCALE, None, ALU.mult)
            e.tensor_scalar(lam_k[:, :, :], lam_k[:, :, :], QKV_SCALE, None, ALU.mult)
            e.wait_ge(s_mask, 1)
            e.tensor_scalar(mask[:, :, :], mask[:, :, :], SCORE_SCALE, None, ALU.mult).then_inc(s_tab, 1)
            for it in FIRST_TILES[5:]:
                vector_item(e, it, -1)
            for n in range(len(pieces) + 1):
                if n < len(pieces):
                    e.wait_ge(ld_piece[n % 3], 16 * (n // 3 + 1))
                    e.tensor_reduce(pm[:, n:n + 1], slot(n), axis=AX.XY, op=ALU.max,
                                    apply_absolute_value=True).then_inc(s_red, 1)
                if n:
                    m = n - 1
                    e.wait_ge(s_all, m + 1)
                    power(m, m + 1)
                    e.tensor_scalar(ws[:, m:m + 1], ip[:, m:m + 1], 2.0 ** 14, None, ALU.mult).then_inc(s_scale, 1)
                    e.wait_ge(s_scale, m + 1)
                    hi_part, lo_part = piece_parts(m)
                    e.wait_ge(s_whi, m + 1)
                    e.scalar_tensor_tensor(out=lo_part, in0=slot(m), scalar=ws[:, m:m + 1], in1=hi_part,
                                           op0=ALU.mult, op1=ALU.subtract).then_inc(s_wlo, 1)
            for q in range(NQ):
                g, u, d = 3 * q, 3 * q + 1, 3 * q + 2
                last = e.tensor_scalar(sgate[:, q:q + 1], p2[:, g:g + 1], 2.0 ** -24, None, ALU.mult)
                if q == 0:
                    last.then_inc(ve["CHAIN"].sem, 2)
                e.tensor_scalar(cu[:, q:q + 1], ip[:, g:g + 1], 2.0 ** -29, None, ALU.mult)
                link(e.tensor_scalar(cd[:, q:q + 1], p2[:, g:g + 1], p2[:, u:u + 1], 2.0 ** -9, ALU.mult, ALU.mult))
                e.tensor_scalar(cd[:, q:q + 1], cd[:, q:q + 1], p2[:, d:d + 1], None, ALU.mult).then_inc(s_ffn, 1)
            e.wait_ge(s_ffn, NQ)

            def body(blk):
                chain[0] = 0
                for it in SEQUENCE:
                    vector_item(e, it, blk)
                assert chain[0] == ve["CHAIN"].per

            blocks(e, body, lambda: e.memset(state[:, 0, :, :], 0.0))


def kernel(L0_attn_x, L0_attn_qkv_w, L0_attn_qkv_norm_w, L0_attn_proj_w, L0_attn_proj_norm_w,
           L0_attn_norm_w, L0_attn_s, L0_ffn_w_gate, L0_ffn_w_up, L0_ffn_w_down):
    import concourse.bacc as bacc
    from concourse.bass_utils import run_bass_kernel_spmd

    def a(t):
        return np.asarray(t)

    hidden = lambda w: a(w).T.reshape(KT, P, NQ, HID // NQ).transpose(2, 1, 0, 3)
    arrays = {
        "x": a(L0_attn_x).reshape(TOK, D),
        "qkv_t": a(L0_attn_qkv_w).T.reshape(KT, P, 3 * D).transpose(1, 0, 2).reshape(P, KT * 3 * D),
        "proj_t": a(L0_attn_proj_w).T.reshape(KT, P, D).transpose(1, 0, 2).reshape(P, KT * D),
        "gate_t": hidden(L0_ffn_w_gate),
        "up_t": hidden(L0_ffn_w_up),
        "down_t": a(L0_ffn_w_down).T.reshape(NQ, HPQ, P, D).transpose(0, 2, 1, 3),
        "qn_w": a(L0_attn_qkv_norm_w), "on_w": a(L0_attn_norm_w), "pn_w": a(L0_attn_proj_norm_w),
        "s_row": a(L0_attn_s),
        "s_part": np.repeat(a(L0_attn_s).reshape(GROUPS, HPG).T, HD, axis=0),
    }
    arrays = {n: np.ascontiguousarray(t) for n, t in arrays.items()}
    nc = bacc.Bacc("TRN2", target_bir_lowering=False, num_devices=1)
    aps = [nc.dram_tensor(n, t.shape, mybir.dt.from_np(t.dtype), kind="ExternalInput").ap() for n, t in arrays.items()]
    out = nc.dram_tensor("out", (TOK, D), F32, kind="ExternalOutput").ap()
    build(nc, *aps, out)
    r = run_bass_kernel_spmd(nc, [arrays], core_ids=[0])
    return r.results[0]["out"].reshape(BATCH, SEQ, D)
```

```python
import numpy as np
import concourse.bass as bass
from concourse import mybir

F32, F16, U32, I32 = mybir.dt.float32, mybir.dt.float16, mybir.dt.uint32, mybir.dt.int32
ALU = mybir.AluOpType
ACT = mybir.ActivationFunctionType
AX = mybir.AxisListType

P = 128
D = 512
KT = D // P
HEADS, HD = 16, 32
HPG = P // HD
GROUPS = HEADS // HPG
BATCH, SEQ = 4, 1024
TOK = BATCH * SEQ
BLK = 512
TPB = BLK // P
BPB = SEQ // BLK
NBLK = TOK // BLK
HALF = 2 * P
HID = 2048
HT = HID // P
NQ = 4
HPQ = HT // NQ
STEPS = 2 * GROUPS
SMALL = 276

LN_EPS, RMS_EPS, OUT_EPS = 1e-5, float(np.finfo(np.float32).eps), 1e-6
MAGIC = 1.5 * 2.0 ** 23
LEAST = 1e-12
X_SCALE = 2.0 ** 10
H_SCALE = 2.0 ** 9
QKV_SCALE = 2.0 ** -4
SCORE_SCALE = 2.0 ** -20
QL_SCALE = 2.0 ** -24
OUT_UNIT = 2.0 ** 32


class Count:

    def __init__(self, nc, name, per, before=0):
        self.sem, self.per, self.before = nc.alloc_semaphore(name), per, before

    def at(self, blk, k):
        if isinstance(blk, int):
            return self.before + self.per * blk + k
        return blk * self.per + (self.before + k)


def schedule():
    tiles = [[(kind, h) for h in range(HPQ * q, HPQ * (q + 1)) for kind in ("G", "U")] for q in range(NQ)]
    down = [[("D", q, c) for c in range(TPB)] for q in range(NQ)]

    def mix(q):
        return [x for n in range(TPB) for x in (*tiles[q][2 * n:2 * n + 2], down[q - 1][n])]

    fill = iter(tiles[0] + mix(1) + mix(2) + tiles[3] + down[2] + down[3])

    def f(n=1):
        return [next(fill) for _ in range(n)]

    seq = [("V", 0), ("V", 1), ("Q", 0), ("K", 0)]
    for s in range(STEPS):
        after = s == GROUPS
        seq += f() + [("SC", s, 0), ("KT", s)]
        seq += [("NR", 0)] * after + f() + [("ZT", 0)] * after + f()
        seq += [("KV", s), ("O", s, 0)] + [("PJ", 0), ("ZT", 1)] * after + [("SC", s, 1)]
        if s + 1 < STEPS:
            seq += [("Q", s + 1), ("K", s + 1)]
        if s + 1 == STEPS:
            seq += [("ST", 0)]
        seq += f() + [("PJ", 1)] * after + f() + [("O", s, 1)]
        if s + 1 == GROUPS:
            seq += [("V", 2), ("NA", 0), ("V", 3), ("NA", 1)]
    seq += f() + [("TX", 0), ("TX", 1), ("NA", 2)] + f() + [("NA", 3)] + f() + [("TH", 0), ("TH", 1), ("NR", 1)]
    seq += f() + [("ZT", 2), ("ST", 1)] + f() + [("PJ", 2), ("ZT", 3), ("TX", 2), ("TX", 3)]
    seq += f() + [("PJ", 3)] + f() + [("TH", 2), ("TH", 3)] + f()
    assert not list(fill)
    return seq


def with_weights(seq):
    at = {n: [] for n in range(NQ * (2 * HPQ + TPB))}
    for piece, ns in PIECE_FILLS.items():
        for kind, n in zip(("WA", "WB", "WC"), ns):
            at[n].append((kind, piece))
    out, fills = [], 0
    for it in seq:
        out += {("V", 0): [("WA", 0), ("WA", 1)], ("V", 1): [("WN", 0)],
                ("Q", 0): [("WB", 0), ("WB", 1), ("WC", 0), ("WP", 0)], ("G", 0): [("WC", 1)]}.get(it, [])
        if it[0] in ("G", "U", "D"):
            out += sorted(at[fills], key=lambda x: x[1])
            fills += 1
        out.append(it)
    for q in range(NQ):
        for kind, it in (("gate", ("G", HPQ * q)), ("up", ("U", HPQ * q)), ("down", ("D", q, 0))):
            assert out.index(("WC", PIECES.index((kind, q)))) < out.index(it), (kind, q)
    for n in range(2, len(PIECES)):
        assert out.index(("WC", n - 2)) < out.index(("WA", n)), n
    return out


SEQUENCE = schedule()
PIECES = [("gate", 0), ("up", 0), ("gate", 1), ("up", 1), ("down", 0), ("gate", 2), ("up", 2), ("down", 1),
          ("gate", 3), ("up", 3), ("down", 2), ("down", 3)]
PIECE_FILLS = {2: (1, 3, 4), 3: (3, 5, 7), 4: (6, 8, 10), 5: (8, 10, 12), 6: (13, 15, 17), 7: (16, 18, 20), 8: (21, 23, 25), 9: (25, 27, 29), 10: (30, 32, 34), 11: (35, 37, 39)}
SEQUENCE_0 = with_weights(SEQUENCE)
FIRST_TILES = [("ST", 0), ("TX", 0), ("TX", 1), ("TH", 0), ("TH", 1),
               ("ST", 1), ("TX", 2), ("TX", 3), ("TH", 2), ("TH", 3)]
DVE_PIECES = 5
Y_ADDS = [it for it in SEQUENCE if it[0] in ("D", "PJ")]
POOLED = [it for it in SEQUENCE if it[0] in ("V", "Q", "K", "KT", "KV", "ZT", "PJ", "TX", "TH", "D")]
N_SHARED = 4
assert len(POOLED) % N_SHARED == 0


def build(nc, x, qkv_t, proj_t, gate_t, up_t, down_t, qn_w, on_w, pn_w, s_row, s_part, out, spill):
    def sb(name, shape, dt):
        return nc.alloc_sbuf_tensor(name, shape, dt)

    wg = [sb(f"wg_{n}", [P, KT, HID], F16) for n in ("hi", "lo")]
    wu = [sb(f"wu_{n}", [P, KT, HID], F16) for n in ("hi", "lo")]
    wd = [sb(f"wd_{n}", [P, HT, D], F16) for n in ("hi", "lo")]
    wq = sb("wq", [P, KT, 3 * D], F16)
    wp = sb("wp", [P, KT, D], F16)
    stage = sb("stage", [P, 2, 4, 512], F32)
    arena = sb("arena", [P, 8192], F32)
    gated = [[arena[:, 2048 * b + 1024 * n:2048 * b + 1024 * (n + 1)].bitcast(F16)
              .rearrange("p (t n) -> p t n", t=HPQ) for n in range(2)] for b in range(2)]
    y = arena[:, 4096:6144].rearrange("p (c n) -> p c n", c=TPB)
    o = arena[:, 6144:7168].rearrange("p (c n) -> p c n", c=2)
    osq = arena[:, 7168:7680]
    z = [arena[:, 7680 + 256 * n:7936 + 256 * n].bitcast(F16).rearrange("p (k t) -> p k t", k=KT)
         for n in range(2)]
    xt = [sb(f"xt_{n}", [P, KT, BLK], F16) for n in ("hi", "lo")]
    ht = [sb(f"ht_{n}", [P, KT, BLK], F16) for n in ("hi", "lo")]
    xin = sb("xin", [P, 2, D], F32)
    v = [sb(f"v_{n}", [P, 2, D], F16) for n in ("hi", "lo")]
    qb = [sb(f"qb_{n}", [P, 2, HPG, P], F16) for n in ("hi", "lo")]
    kf = [sb(f"kf_{n}", [P, HALF], F16) for n in ("hi", "lo")]
    ql = sb("ql", [P, 2, HALF], F32)
    kl = sb("kl", [P, HALF], F32)
    kt = [sb(f"kt_{n}", [P, HALF], F16) for n in ("hi", "lo")]
    kvm = kl[:, :].rearrange("p (c t) -> p c t", c=2)
    state = sb("state", [P, 2, GROUPS, P], F32)
    state1 = sb("state1", [P, P], F32)
    sm = sb("sm", [P, HPG, P], F32)
    smp = [sb(f"sm_{n}", [P, HPG, P], F16) for n in ("hi", "lo")]
    sg = sb("sg", [P, BLK], F32)
    ramp_diff, ramp, ramp_back = sm[:, 2, :], sm[:, 3, :], sg[:, 0:P]
    x_late = wd[0][:, 3 * HPQ:4 * HPQ, :].rearrange("p i n -> p (i n)").bitcast(F32).rearrange("p (c n) -> p c n", c=2)
    max_row = [x_late[:, n % 8 // 4, P * (n % 4):P * (n % 4 + 1)] for n in range(len(PIECES))]
    mask = sb("mask", [P, HEADS, P], F32)
    lam_q = sb("lam_q", [P, GROUPS, P], F32)
    lam_k = sb("lam_k", [P, GROUPS, P], F32)
    diag = sb("diag", [P, P], F32)
    qn_b = sb("qn_b", [P, D], F32)
    on2_b = sb("on2_b", [P, D], F32)
    op_b = sb("op_b", [P, D], F32)
    ident = sb("ident", [P, P], F32)
    small, used = sb("small", [P, SMALL], F32), [0]

    def table(*shape):
        start = used[0]
        used[0] += int(np.prod(shape))
        assert used[0] <= SMALL
        flat = small[:, start:used[0]]
        return flat if len(shape) == 1 else flat.rearrange("p (a b) -> p a b", a=shape[0])

    sr = table(HEADS)
    sp = table(GROUPS)
    head = table(4, HEADS)
    part = table(6, GROUPS)
    pm = table(16)
    am = table(16)
    p2 = table(16)
    ip = table(16)
    ws = table(16)
    sgate = table(NQ)
    cu = table(NQ)
    cd = table(NQ)
    keep = table(2, NBLK)
    beta = table(16)
    st6 = table(2, 6)
    idle = table(1)
    mv = table(2, 2)
    var_ab = table(3, 2)
    rs = table(2, 2)
    mhalf = table(4)
    nrm = table(5, 2)

    banks = [nc.alloc_psum_tensor(f"bank{n}", [P, 512], F32) for n in range(8)]
    b_gate, b_up, b_sc, b_o = banks[0], banks[1], banks[2], banks[3]
    shared = banks[4:8]

    def bank_of(it):
        return shared[POOLED.index(it) % N_SHARED]

    C = lambda name, per, before=0: Count(nc, name, per, before)
    pe = {k: C("pe_" + k, n, b) for k, n, b in (
        ("V", 4, 0), ("Q", 8, 0), ("K", 8, 0), ("KT", 8, 0), ("KV", 8, 0), ("SC", 16, 0), ("O", 16, 0),
        ("ZT", 4, 1), ("PJ", 4, 0), ("TX", 4, 4), ("TH", 4, 4), ("G", 16, 0), ("U", 16, 0), ("D", 16, 0))}
    ac = {k: C("act_" + k, n, b) for k, n, b in (
        ("V", 4, 0), ("Q", 8, 0), ("K", 8, 0), ("KT", 8, 0), ("SM", 16, 0), ("SQ", 4, 0), ("Z", 4, 0),
        ("TX", 4, 4), ("TH", 4, 4), ("SILU", 16, 1), ("GH", 16, 0))}
    ve = {k: C("dve_" + k, n, b) for k, n, b in (
        ("V", 4, 0), ("Q", 8, 1), ("K", 8, 1), ("KT", 8, 1), ("KVM", 8, 1), ("S1", 8, 0), ("S2", 8, 0),
        ("SM", 16, 1), ("SL", 16, 0), ("OUT", 8, 1), ("SUM", 4, 1), ("U", 2, 0), ("ZN", 4, 0), ("Z", 4, 1),
        ("Y", 20, 21), ("XN", 4, 4), ("H", 4, 4), ("TX", 4, 4), ("TH", 4, 4), ("VAR", 2, 2),
        ("GT", 16, 1), ("GL", 16, 1), ("CHAIN", 12, 12), ("KEEP", 1, 0))}
    po = {k: C("pool_" + k, n, b) for k, n, b in (("RS", 2, 2), ("R", 2, 0))}
    ld_x = [C(f"ld_x{n}", 32) for n in range(2)]
    ld_y, st_y = C("ld_y", 16), C("st_y", 64, 16)

    def sem(name):
        return nc.alloc_semaphore(name)

    ld_qn, ld_on, ld_first = sem("ld_qn"), sem("ld_on"), [sem(f"ld_first{c}") for c in range(TPB)]
    ld_tab, ld_proj = sem("ld_tab"), sem("ld_proj")
    ld_qkv = [sem(f"ld_qkv{n}") for n in range(KT)]
    ld_piece = [sem(f"ld_piece{n}") for n in range(2)]
    s_ident, s_pool, s_arg, s_exp, s_mask, s_tab = (sem(n) for n in (
        "ident", "pool_chain", "exponents", "exp", "masked", "tables"))
    s_pro, s_sum, s_tern, s_red, s_all, s_scale, s_whi, s_ones, s_abs, s_clip, s_spill = (sem(n) for n in (
        "pro_chain", "beta_sum", "ternary", "piece_max", "piece_allmax", "piece_scale", "piece_hi",
        "beta_total", "beta_part", "clipped", "max_spilled"))
    s_wlo = {"dve": sem("piece_lo_dve"), "pool": sem("piece_lo_pool")}

    dram = {"gate": gate_t, "up": up_t, "down": down_t}

    def slot(n):
        return stage[:, n % 2, :, :]

    def piece_parts(n):
        kind, q = PIECES[n]
        if kind == "down":
            return [w[:, HPQ * q:HPQ * (q + 1), :] for w in wd]
        return [w[:, :, 512 * q:512 * (q + 1)] for w in (wg if kind == "gate" else wu)]

    def cut(n):
        return (s_wlo["dve"], n + 1) if n < DVE_PIECES else (s_wlo["pool"], n + 1 - DVE_PIECES)

    def raw(c):
        if c < KT:
            return arena[:, 3 * D * c:3 * D * (c + 1)], wq[:, c, :]
        return arena[:, 6144:8192], wp[:, :, :].rearrange("p k n -> p (k n)")

    def x_tile(blk, c):
        return x_late[:, c % 2, :] if ahead(blk) and c >= 2 else xin[:, c % 2, :]

    def ahead(blk):
        return isinstance(blk, int) and blk < 0

    def shared_free(it, blk, executed):
        order = [i for i in POOLED if i in executed]
        n, at = order.index(it), bank_of(it)
        for back in range(1, len(order) + 1):
            other = order[n - back]
            if bank_of(other) is at:
                wrapped = n - back < 0
                break
        if wrapped and ahead(blk):
            return None
        cnt, k = {"D": lambda: (ve["Y"], Y_ADDS.index(other) + 1), "PJ": lambda: (ve["Y"], Y_ADDS.index(other) + 1),
                  "ZT": lambda: (ve["Z"], other[1] + 1), "KV": lambda: (ve["KVM"], other[1] + 1),
                  }.get(other[0], lambda: (ve[other[0]], other[1] + 1))()
        return cnt.sem, cnt.at(blk, k - (cnt.per if wrapped else 0))

    def tensor_item(e, it, blk, executed):
        kind = it[0]
        if kind in ("V", "Q", "K", "KT", "KV", "ZT", "PJ", "TX", "TH", "D"):
            free = shared_free(it, blk, executed)
            if free:
                e.wait_ge(*free)
            bank = bank_of(it)

        def products(dst, lhs, rhs, start=True, stop=True):
            for n, (a, b) in enumerate(zip(lhs, rhs)):
                last = e.matmul(dst, a, b, start=start and n == 0, stop=stop and n == len(lhs) - 1)
            return last

        if kind == "V":
            c = it[1]
            e.wait_ge(ve["TH"].sem, ve["TH"].at(blk, c + 1 - 4))
            t = slice(P * c, P * (c + 1))
            products(bank[:, :], [ht[n][:, k, t] for k in range(KT) for n in range(2)],
                     [wq[:, k, 2 * D:3 * D] for k in range(KT) for n in range(2)]).then_inc(pe["V"].sem, 1)
        elif kind in ("Q", "K"):
            s = it[1]
            a, j = divmod(s, GROUPS)
            e.wait_ge(ve["TH"].sem, ve["TH"].at(blk, 2 * a + 2 - 4))
            f = (D if kind == "K" else 0) + P * j
            products(bank[:, 0:HALF], [wq[:, k, f:f + P] for k in range(KT) for n in range(2)],
                     [ht[n][:, k, HALF * a:HALF * (a + 1)] for k in range(KT) for n in range(2)])\
                .then_inc(pe[kind].sem, 1)
        elif kind == "KT":
            s = it[1]
            e.wait_ge(ve["K"].sem, ve["K"].at(blk, s + 1))
            for c in range(2):
                last = e.transpose(bank[:, P * c:P * (c + 1)], kl[:, P * c:P * (c + 1)], ident[:, :])
            last.then_inc(pe["KT"].sem, 1)
        elif kind == "SC":
            _, s, c = it
            e.wait_ge(ve["K"].sem, ve["K"].at(blk, s + 1))
            e.wait_ge(ve["SM"].sem, ve["SM"].at(blk, 2 * s + c))
            t = slice(P * c, P * (c + 1))
            products(b_sc[:, :], [kf[0][:, t], kf[0][:, t], kf[1][:, t]],
                     [qb[n][:, c, :, :] for n in (0, 1, 0)]).then_inc(pe["SC"].sem, 1)
        elif kind == "KV":
            s = it[1]
            j = s % GROUPS
            e.wait_ge(ve["KT"].sem, ve["KT"].at(blk, s + 1))
            e.wait_ge(ve["V"].sem, ve["V"].at(blk, 2 * (s // GROUPS) + 2))
            for c in range(2):
                t, f = slice(P * c, P * (c + 1)), slice(P * j, P * (j + 1))
                last = products(bank[:, t], [kt[0][:, t], kt[0][:, t], kt[1][:, t]],
                                [v[n][:, c, f] for n in (0, 1, 0)])
            last.then_inc(pe["KV"].sem, 1)
        elif kind == "O":
            _, s, c = it
            a, j = divmod(s, GROUPS)
            e.wait_ge(ve["SL"].sem, ve["SL"].at(blk, 2 * s + c + 1))
            if c == 0:
                e.wait_ge(ve["OUT"].sem, ve["OUT"].at(blk, s))
                cross = state[:, a, j, :]
            else:
                e.wait_ge(ve["S1"].sem, ve["S1"].at(blk, s + 1))
                cross = state1[:, :]
            products(b_o[:, P * c:P * (c + 1)], [ql[:, s % 2, P * c:P * (c + 1)]], [cross], stop=False)
            for h in range(HPG):
                f = slice(P * j + HD * h, P * j + HD * (h + 1))
                last = products(b_o[:, P * c + HD * h:P * c + HD * (h + 1)],
                                [smp[0][:, h, :], smp[0][:, h, :], smp[1][:, h, :]],
                                [v[n][:, c, f] for n in (0, 1, 0)], start=False, stop=h == HPG - 1)
            last.then_inc(pe["O"].sem, 1)
        elif kind == "ZT":
            c = it[1]
            e.wait_ge(ve["ZN"].sem, ve["ZN"].at(blk, c + 1))
            for k in range(KT):
                last = e.transpose(bank[:, P * k:P * (k + 1)], o[:, c % 2, P * k:P * (k + 1)], ident[:, :])
            last.then_inc(pe["ZT"].sem, 1)
        elif kind == "PJ":
            c = it[1]
            if c == 0:
                e.wait_ge(s_tern, KT + 1)
            e.wait_ge(ve["Z"].sem, ve["Z"].at(blk, c + 1))
            products(bank[:, :], [z[n][:, k, :] for k in range(KT) for n in range(2)],
                     [wp[:, k, :] for k in range(KT) for n in range(2)]).then_inc(pe["PJ"].sem, 1)
        elif kind in ("TX", "TH"):
            c = it[1]
            made = ve["XN" if kind == "TX" else "H"]
            e.wait_ge(made.sem, made.at(blk, c + 1))
            for k in range(KT):
                last = e.transpose(bank[:, P * k:P * (k + 1)], x_tile(blk, c)[:, P * k:P * (k + 1)], ident[:, :])
            last.then_inc(pe[kind].sem, 1)
        elif kind in ("G", "U"):
            h = it[1]
            if (kind, h) == ("G", 0):
                e.wait_ge(ve["TX"].sem, ve["TX"].at(blk, 0))
            if h % HPQ == 0:
                e.wait_ge(*cut(PIECES.index(("gate" if kind == "G" else "up", h // HPQ))))
            t = slice(P * h, P * (h + 1))
            w, bank, free = (wg, b_gate, ac["SILU"]) if kind == "G" else (wu, b_up, ve["GT"])
            e.wait_ge(free.sem, free.at(blk, h))
            products(bank[:, :], [w[n][:, k, t] for k in range(KT) for n in (0, 0, 1)],
                     [xt[n][:, k, :] for k in range(KT) for n in (0, 1, 0)]).then_inc(pe[kind].sem, 1)
        elif kind == "D":
            _, q, c = it
            e.wait_ge(ve["GL"].sem, ve["GL"].at(blk, HPQ * (q + 1)))
            if c == 0:
                e.wait_ge(*cut(PIECES.index(("down", q))))
            g, t = gated[q % 2], slice(P * c, P * (c + 1))
            products(bank[:, :], [g[n][:, i, t] for i in range(HPQ) for n in (0, 0, 1)],
                     [wd[n][:, HPQ * q + i, :] for i in range(HPQ) for n in (0, 1, 0)]).then_inc(pe["D"].sem, 1)

    def scalar_item(e, it, blk):
        kind = it[0]
        if kind == "V":
            e.wait_ge(pe["V"].sem, pe["V"].at(blk, it[1] + 1))
            e.activation(v[0][:, it[1] % 2, :], bank_of(it)[:, :], ACT.Copy, scale=QKV_SCALE).then_inc(ac["V"].sem, 1)
        elif kind == "Q":
            e.wait_ge(pe["Q"].sem, pe["Q"].at(blk, it[1] + 1))
            for h in range(HPG):
                r = slice(HD * h, HD * (h + 1))
                last = e.activation(qb[0][r, :, h, :], bank_of(it)[r, 0:HALF].rearrange("p (c t) -> p c t", c=2),
                                    ACT.Copy, scale=QKV_SCALE)
            last.then_inc(ac["Q"].sem, 1)
        elif kind == "K":
            e.wait_ge(pe["K"].sem, pe["K"].at(blk, it[1] + 1))
            e.activation(kf[0][:, :], bank_of(it)[:, 0:HALF], ACT.Copy, scale=QKV_SCALE).then_inc(ac["K"].sem, 1)
        elif kind == "KT":
            e.wait_ge(pe["KT"].sem, pe["KT"].at(blk, it[1] + 1))
            e.activation(kt[0][:, :], bank_of(it)[:, 0:HALF], ACT.Copy).then_inc(ac["KT"].sem, 1)
        elif kind == "SC":
            _, s, c = it
            e.wait_ge(ve["SM"].sem, ve["SM"].at(blk, 2 * s + c + 1))
            e.activation(smp[0][:, :, :], sm[:, :, :], ACT.Copy).then_inc(ac["SM"].sem, 1)
        elif kind == "NA":
            c = it[1]
            e.wait_ge(ve["OUT"].sem, ve["OUT"].at(blk, 4 * (c // 2) + 4))
            e.wait_ge(ve["SUM"].sem, ve["SUM"].at(blk, c))
            e.activation(osq[:, :], o[:, c % 2, :], ACT.Square, accum_out=nrm[:, 0, c % 2:c % 2 + 1])\
                .then_inc(ac["SQ"].sem, 1)
        elif kind == "ZT":
            c = it[1]
            e.wait_ge(pe["ZT"].sem, pe["ZT"].at(blk, c + 1))
            e.activation(z[0][:, :, :], bank_of(it)[:, :].rearrange("p (k t) -> p k t", k=KT), ACT.Copy)\
                .then_inc(ac["Z"].sem, 1)
        elif kind in ("TX", "TH"):
            c = it[1]
            dst, scale = (xt, X_SCALE) if kind == "TX" else (ht, 1.0)
            e.wait_ge(pe[kind].sem, pe[kind].at(blk, c + 1))
            e.activation(dst[0][:, :, P * c:P * (c + 1)], bank_of(it)[:, :].rearrange("p (k t) -> p k t", k=KT),
                         ACT.Copy, scale=scale).then_inc(ac[kind].sem, 1)
        elif kind == "G":
            h = it[1]
            q = h // HPQ
            e.wait_ge(pe["G"].sem, pe["G"].at(blk, h + 1))
            e.wait_ge(ve["GL"].sem, ve["GL"].at(blk, h))
            e.activation(sg[:, :], b_gate[:, :], ACT.Silu, scale=sgate[:, q:q + 1]).then_inc(ac["SILU"].sem, 1)
        elif kind == "U":
            h = it[1]
            q = h // HPQ
            e.wait_ge(ve["GT"].sem, ve["GT"].at(blk, h + 1))
            e.activation(gated[q % 2][0][:, h % HPQ, :], sg[:, :], ACT.Copy).then_inc(ac["GH"].sem, 1)

    chain = [0]

    def vector_item(e, it, blk):
        kind = it[0]

        def lo(dst, src, scale, hi, ready, k):
            e.wait_ge(ready.sem, ready.at(blk, k))
            if scale == 1.0:
                return e.tensor_tensor(dst, src, hi, ALU.subtract)
            return e.scalar_tensor_tensor(out=dst, in0=src, scalar=scale, in1=hi, op0=ALU.mult, op1=ALU.subtract)

        def link(ins):
            chain[0] += 1
            ins.then_inc(ve["CHAIN"].sem, 1)
            e.wait_ge(ve["CHAIN"].sem, ve["CHAIN"].at(blk, chain[0]))

        if kind == "V":
            c = it[1] % 2
            lo(v[1][:, c, :], bank_of(it)[:, :], QKV_SCALE, v[0][:, c, :], ac["V"], it[1] + 1).then_inc(ve["V"].sem, 1)
        elif kind == "Q":
            s = it[1]
            b = bank_of(it)
            for h in range(HPG):
                r = slice(HD * h, HD * (h + 1))
                lo(qb[1][r, :, h, :], b[r, 0:HALF].rearrange("p (c t) -> p c t", c=2), QKV_SCALE,
                   qb[0][r, :, h, :], ac["Q"], s + 1)
            e.tensor_tensor(ql[:, s % 2, :].rearrange("p (c t) -> p c t", c=2),
                            b[:, 0:HALF].rearrange("p (c t) -> p c t", c=2),
                            lam_q[:, s % GROUPS, :].unsqueeze(1).to_broadcast([P, 2, P]), ALU.mult)\
                .then_inc(ve["Q"].sem, 1)
        elif kind == "K":
            s = it[1]
            b = bank_of(it)
            lo(kf[1][:, :], b[:, 0:HALF], QKV_SCALE, kf[0][:, :], ac["K"], s + 1)
            e.tensor_tensor(kl[:, :].rearrange("p (c t) -> p c t", c=2),
                            b[:, 0:HALF].rearrange("p (c t) -> p c t", c=2),
                            lam_k[:, s % GROUPS, :].unsqueeze(1).to_broadcast([P, 2, P]), ALU.mult)\
                .then_inc(ve["K"].sem, 1)
        elif kind == "KT":
            s = it[1]
            lo(kt[1][:, :], bank_of(it)[:, 0:HALF], 1.0, kt[0][:, :], ac["KT"], s + 1).then_inc(ve["KT"].sem, 1)
        elif kind == "SC":
            _, s, c = it
            j, k = s % GROUPS, 2 * s + c + 1
            e.wait_ge(pe["SC"].sem, pe["SC"].at(blk, k))
            e.tensor_tensor(sm[:, :, :], b_sc[:, :].rearrange("p (h t) -> p h t", h=HPG),
                            mask[:, HPG * j:HPG * (j + 1), :], ALU.mult).then_inc(ve["SM"].sem, 1)
            lo(smp[1][:, :, :], sm[:, :, :], 1.0, smp[0][:, :, :], ac["SM"], k).then_inc(ve["SL"].sem, 1)
        elif kind == "KV":
            s = it[1]
            a, j = divmod(s, GROUPS)
            e.wait_ge(pe["KV"].sem, pe["KV"].at(blk, s + 1))
            e.scalar_tensor_tensor(out=kvm, in0=bank_of(it)[:, 0:HALF].rearrange("p (c t) -> p c t", c=2),
                                   scalar=part[:, 5, j:j + 1], in1=diag[:, :].unsqueeze(1).to_broadcast([P, 2, P]),
                                   op0=ALU.mult, op1=ALU.mult).then_inc(ve["KVM"].sem, 1)
            e.wait_ge(ve["KVM"].sem, ve["KVM"].at(blk, s + 1))
            e.scalar_tensor_tensor(out=state1[:, :], in0=state[:, a, j, :], scalar=part[:, 4, j:j + 1],
                                   in1=kvm[:, 0, :], op0=ALU.mult, op1=ALU.add).then_inc(ve["S1"].sem, 1)
            e.wait_ge(ve["S1"].sem, ve["S1"].at(blk, s + 1))
            e.scalar_tensor_tensor(out=state[:, 1 - a, j, :], in0=state1[:, :], scalar=part[:, 4, j:j + 1],
                                   in1=kvm[:, 1, :], op0=ALU.mult, op1=ALU.add).then_inc(ve["S2"].sem, 1)
        elif kind == "O":
            _, s, c = it
            if c == 0:
                return
            a, j = divmod(s, GROUPS)
            e.wait_ge(pe["O"].sem, pe["O"].at(blk, 2 * s + 2))
            e.wait_ge(pe["ZT"].sem, pe["ZT"].at(blk, 2 * a))
            e.tensor_tensor(o[:, :, P * j:P * (j + 1)].rearrange("p c (h d) -> p c h d", h=HPG),
                            b_o[:, 0:HALF].rearrange("p (c h d) -> p c h d", c=2, h=HPG),
                            head[:, 3, HPG * j:HPG * (j + 1)].unsqueeze(1).unsqueeze(3).to_broadcast([P, 2, HPG, HD]),
                            ALU.mult).then_inc(ve["OUT"].sem, 1)
        elif kind == "NA":
            c = it[1]
            e.wait_ge(ac["SQ"].sem, ac["SQ"].at(blk, c + 1))
            e.tensor_tensor_reduce(out=osq[:, :], in0=osq[:, :], in1=on2_b[:, :], scale=1.0, scalar=0.0,
                                   op0=ALU.mult, op1=ALU.add, accum_out=nrm[:, 1, c % 2:c % 2 + 1])\
                .then_inc(ve["SUM"].sem, 1)
        elif kind == "NR":
            a = it[1]
            e.wait_ge(ve["SUM"].sem, ve["SUM"].at(blk, 2 * a + 2))
            link(e.tensor_scalar(nrm[:, 2, :], nrm[:, 0, :], RMS_EPS / D, RMS_EPS * OUT_EPS, ALU.mult, ALU.add))
            e.scalar_tensor_tensor(out=nrm[:, 3, :], in0=nrm[:, 1, :], scalar=1.0 / D, in1=nrm[:, 2, :],
                                   op0=ALU.mult, op1=ALU.add).then_inc(ve["U"].sem, 1)
            e.wait_ge(po["R"].sem, po["R"].at(blk, a + 1))
            for c in range(2):
                e.scalar_tensor_tensor(out=o[:, c, :], in0=o[:, c, :], scalar=nrm[:, 4, c:c + 1], in1=op_b[:, :],
                                       op0=ALU.mult, op1=ALU.mult).then_inc(ve["ZN"].sem, 1)
        elif kind == "ZT":
            c = it[1]
            lo(z[1][:, :, :], bank_of(it)[:, :].rearrange("p (k t) -> p k t", k=KT), 1.0, z[0][:, :, :],
               ac["Z"], c + 1).then_inc(ve["Z"].sem, 1)
        elif kind in ("PJ", "D"):
            c, k = it[-1], Y_ADDS.index(it)
            if all(i[-1] != c for i in Y_ADDS[:k]):
                e.wait_ge(ld_y.sem, ld_y.at(blk, 16))
            mine, n = (pe["PJ"], c + 1) if kind == "PJ" else (pe["D"], TPB * it[1] + c + 1)
            e.wait_ge(mine.sem, mine.at(blk, n))
            e.wait_ge(ve["Y"].sem, ve["Y"].at(blk, k))
            e.scalar_tensor_tensor(out=y[:, c, :], in0=bank_of(it)[:, :],
                                   scalar=beta[:, 8:9] if kind == "PJ" else cd[:, it[1]:it[1] + 1],
                                   in1=y[:, c, :], op0=ALU.mult, op1=ALU.add).then_inc(ve["Y"].sem, 1)
        elif kind == "ST":
            p = it[1]
            for c in range(2):
                if ahead(blk):
                    e.wait_ge(ld_first[2 * p + c], 16)
                else:
                    e.wait_ge(ld_x[c].sem, ld_x[c].at(blk, 16 * (p + 1)))
                last = e.bn_stats(st6[:, c, :], x_tile(blk, 2 * p + c))
            link(last)
            e.memset(idle[:, :], 0.0)
            for c in range(2):
                last = e.bn_aggr(mv[:, c, :], st6[:, c, :])
            link(last)
            link(e.tensor_scalar(var_ab[:, 0, :], mv[:, :, 1], LN_EPS, None, ALU.add))
            link(e.reciprocal(var_ab[:, 2, :], var_ab[:, 0, :]))
            link(e.tensor_tensor(var_ab[:, 2, :], var_ab[:, 2, :], mv[:, :, 1], ALU.mult))
            e.tensor_scalar(var_ab[:, 1, :], var_ab[:, 2, :], RMS_EPS, None, ALU.add).then_inc(ve["VAR"].sem, 1)
            e.wait_ge(po["RS"].sem, po["RS"].at(blk, p + 1))
            for c in range(2):
                t = x_tile(blk, 2 * p + c)
                e.tensor_scalar(t, t, mv[:, c, 0:1], rs[:, 0, c:c + 1],
                                ALU.subtract, ALU.mult).then_inc(ve["XN"].sem, 1)
        elif kind == "TX":
            c = it[1]
            lo(xt[1][:, :, P * c:P * (c + 1)], bank_of(it)[:, :].rearrange("p (k t) -> p k t", k=KT), X_SCALE,
               xt[0][:, :, P * c:P * (c + 1)], ac["TX"], c + 1).then_inc(ve["TX"].sem, 1)
            t = x_tile(blk, c)
            e.scalar_tensor_tensor(out=t, in0=t, scalar=rs[:, 1, c % 2:c % 2 + 1],
                                   in1=qn_b[:, :], op0=ALU.mult, op1=ALU.mult).then_inc(ve["H"].sem, 1)
        elif kind == "TH":
            c = it[1]
            lo(ht[1][:, :, P * c:P * (c + 1)], bank_of(it)[:, :].rearrange("p (k t) -> p k t", k=KT), 1.0,
               ht[0][:, :, P * c:P * (c + 1)], ac["TH"], c + 1).then_inc(ve["TH"].sem, 1)
        elif kind == "U":
            h = it[1]
            q = h // HPQ
            e.wait_ge(pe["U"].sem, pe["U"].at(blk, h + 1))
            e.wait_ge(ac["SILU"].sem, ac["SILU"].at(blk, h + 1))
            e.scalar_tensor_tensor(out=sg[:, :], in0=b_up[:, :], scalar=cu[:, q:q + 1], in1=sg[:, :],
                                   op0=ALU.mult, op1=ALU.mult).then_inc(ve["GT"].sem, 1)
            lo(gated[q % 2][1][:, h % HPQ, :], sg[:, :], 1.0, gated[q % 2][0][:, h % HPQ, :], ac["GH"], h + 1)\
                .then_inc(ve["GL"].sem, 1)

    def pool_item(e, it, blk):
        if it[0] == "ST":
            e.wait_ge(ve["VAR"].sem, ve["VAR"].at(blk, it[1] + 1))
            e.tensor_tensor(rs[:, :, :], var_ab[:, 0:2, :], mhalf[:, :].rearrange("p (a b) -> p a b", a=2), ALU.pow)\
                .then_inc(po["RS"].sem, 1)
        elif it[0] == "NR":
            e.wait_ge(ve["U"].sem, ve["U"].at(blk, it[1] + 1))
            e.tensor_tensor(nrm[:, 4, :], nrm[:, 3, :], mhalf[:, 0:2], ALU.pow).then_inc(po["R"].sem, 1)

    def rows(start, n):
        return slice(start, start + n) if isinstance(start, int) else bass.ds(start, n)

    def load_x(e, blk, row, c):
        if ahead(blk):
            e.dma_start(x_tile(blk, c), x[rows(row + P * c, P), :]).then_inc(ld_first[c], 16)
            return
        e.wait_ge(pe["TH"].sem, pe["TH"].at(blk, c - 1))
        e.dma_start(xin[:, c % 2, :], x[rows(row + P * c, P), :]).then_inc(ld_x[c % 2].sem, 16)

    def blocks(e, body):
        body(0)
        with e.Fori(1, NBLK) as blk:
            body(blk)

    with nc.Block() as block:
        @block.sync
        def _(e):
            e.sem_inc(st_y.sem, st_y.before)
            for c in range(TPB):
                load_x(e, -1, 0, c)
            e.dma_start(qn_b[:, :], qn_w.partition_broadcast(P)).then_inc(ld_qn, 16)
            for c in range(KT):
                e.dma_start(raw(c)[0], qkv_t[:, 1536 * c:1536 * (c + 1)]).then_inc(ld_qkv[c], 16)

            def load_piece(n):
                kind, q = PIECES[n]
                if n >= 2:
                    e.wait_ge(*cut(n - 2))
                e.dma_start(slot(n), dram[kind][q, :, :, :]).then_inc(ld_piece[n % 2], 16)

            e.dma_start(raw(KT)[0], proj_t).then_inc(ld_proj, 16)
            def spread_max(n):
                e.wait_ge(s_red, n + 1)
                e.dma_start(spill[n, :], pm[:, n]).then_inc(s_spill, 16)
                e.wait_ge(s_spill, 16 * (n + 1))
                e.dma_start(max_row[n], spill[n, :].partition_broadcast(P)).then_inc(s_all, 16)

            for n in range(2):
                load_piece(n)
            e.dma_start(on2_b[:, :], on_w.partition_broadcast(P)).then_inc(ld_on, 16)
            e.dma_start(op_b[:, :], pn_w.partition_broadcast(P)).then_inc(ld_on, 16)

            def body(blk):
                if isinstance(blk, int):
                    e.wait_ge(s_tern, KT)
                e.wait_ge(st_y.sem, st_y.at(blk, 0))
                e.dma_start(y[:, :, :], x[rows(blk * BLK, BLK), :].rearrange("(c p) n -> p c n", p=P))\
                    .then_inc(ld_y.sem, 16)
                if isinstance(blk, int):
                    for n in range(len(PIECES)):
                        spread_max(n)
                        if n >= 1 and n + 1 < len(PIECES):
                            load_piece(n + 1)
                row = (blk + 1) % NBLK * BLK
                for c in range(TPB):
                    load_x(e, blk, row, c)
                for c in range(TPB):
                    k = max(n for n, it in enumerate(Y_ADDS) if it[-1] == c) + 1
                    e.wait_ge(ve["Y"].sem, ve["Y"].at(blk, k))
                    e.dma_start(out[rows(blk * BLK + P * c, P), :], y[:, c, :]).then_inc(st_y.sem, 16)

            blocks(e, body)
            e.wait_ge(st_y.sem, st_y.at(NBLK, 0))

        @block.gpsimd
        def _(e):
            done = [0]

            def link(ins):
                done[0] += 1
                ins.then_inc(s_pool, 1)
                e.wait_ge(s_pool, done[0])

            e.memset(ident[:, :], 0.0).then_inc(s_ident, 1)
            e.wait_ge(s_ident, 1)
            e.affine_select(out=ident[:, :], in_=ident[:, :], compare_op=ALU.not_equal, fill=1.0, base=0,
                            pattern=[[-1, P]], channel_multiplier=1).then_inc(s_ident, 1)
            e.memset(mhalf[:, :], -0.5)
            e.iota(sm[:, 0, :].bitcast(I32), [[1, P]], base=0, channel_multiplier=-1)
            link(e.iota(sm[:, 1, :].bitcast(I32), [[1, P]], base=0, channel_multiplier=0))
            e.tensor_scalar(ramp_diff, sm[:, 0, :].bitcast(I32), 0.0, None, ALU.max)
            e.tensor_scalar(ramp_back, sm[:, 1, :].bitcast(I32), -1.0, float(P), ALU.mult, ALU.add)
            e.tensor_copy(ramp, sm[:, 1, :].bitcast(I32))
            e.wait_ge(ld_tab, 32)
            e.tensor_scalar(head[:, 0, :], sr[:, :], -1.0, None, ALU.mult)
            e.tensor_scalar(part[:, 0, :], sp[:, :], -1.0, None, ALU.mult)
            e.tensor_scalar(head[:, 1, :], sr[:, :], 0.0, float(P - 1), ALU.min, ALU.mult)
            e.tensor_scalar(part[:, 1, :], sp[:, :], 0.0, float(P - 1), ALU.min, ALU.mult)
            link(e.tensor_scalar(part[:, 2, :], sp[:, :], 0.0, float(P), ALU.min, ALU.mult))
            pool_item(e, FIRST_TILES[0], -1)
            for j in range(GROUPS):
                e.tensor_scalar(lam_q[:, j, :], ramp, part[:, 0, j:j + 1], part[:, 1, j:j + 1], ALU.mult, ALU.add)
                e.tensor_scalar(lam_k[:, j, :], ramp_back, part[:, 0, j:j + 1], part[:, 2, j:j + 1], ALU.mult, ALU.add)
            for h in range(HEADS):
                last = e.tensor_scalar(mask[:, h, :], ramp_diff, head[:, 0, h:h + 1], head[:, 1, h:h + 1],
                                       ALU.mult, ALU.add)
                if h + 1 == HEADS // 2:
                    pool_item(e, FIRST_TILES[5], -1)
            last.then_inc(s_arg, 1)
            for n in range(2):
                e.memset(qb[n][:, :, :, :].bitcast(U32), 0)
            e.memset(state[:, 0, :, :], 0.0)
            for n in range(NBLK):
                bound = 0.0 if n % BPB == 0 else float(np.finfo(np.float32).max)
                e.memset(keep[:, 0, n:n + 1], -bound)
                e.memset(keep[:, 1, n:n + 1], bound)
            e.wait_ge(s_exp, 1)
            e.affine_select(out=mask[:, :, :], in_=mask[:, :, :], compare_op=ALU.is_ge, fill=0.0, base=0,
                            pattern=[[0, HEADS], [1, P]], channel_multiplier=-1).then_inc(s_mask, 1)

            def body(blk):
                for it in SEQUENCE_0 if isinstance(blk, int) else SEQUENCE:
                    if it[0] == "WP":
                        e.wait_ge(s_clip, KT)
                        w = raw(KT)[0]
                        link(e.tensor_scalar(w, w, beta[:, 5:6], MAGIC, ALU.mult, ALU.add))
                        e.tensor_scalar(w, w, MAGIC + 1.0, MAGIC - 1.0, ALU.min, ALU.max).then_inc(s_clip, 1)
                    elif it[0] == "WC" and it[1] >= DVE_PIECES:
                        e.wait_ge(s_whi, it[1] + 1)
                        hi_part, lo_part = piece_parts(it[1])
                        e.tensor_tensor(lo_part, slot(it[1]), hi_part, ALU.subtract).then_inc(cut(it[1])[0], 1)
                    else:
                        pool_item(e, it, blk)

            blocks(e, body)

        @block.scalar
        def _(e):
            e.sem_inc(ac["SILU"].sem, ac["SILU"].before)
            for dst, src in ((sr[:, :], s_row.partition_broadcast(P)), (sp[:, :], s_part)):
                e.dma_start(dst, src).then_inc(ld_tab, 16)

            def weight_sum(c):
                src, dst = raw(c)
                e.wait_ge(ld_qkv[c] if c < KT else ld_proj, 16)
                e.activation(dst, src, ACT.Abs, accum_out=beta[:, 12 + c:13 + c] if c < KT else beta[:, 1:2])\
                    .then_inc(s_abs, 1)

            def unmagic(c):
                src, dst = raw(c)
                e.wait_ge(s_clip, c + 1)
                e.activation(dst, src, ACT.Copy, bias=-MAGIC).then_inc(s_tern, 1)

            for it in FIRST_TILES[:3]:
                scalar_item(e, it, -1)
            weight_sum(0)
            for it in FIRST_TILES[3:5]:
                scalar_item(e, it, -1)
            weight_sum(1)
            for it in FIRST_TILES[5:8]:
                scalar_item(e, it, -1)
            weight_sum(2)
            for it in FIRST_TILES[8:]:
                scalar_item(e, it, -1)
            e.wait_ge(s_arg, 1)
            e.activation(mask[:, :, :], mask[:, :, :], ACT.Exp).then_inc(s_exp, 1)
            e.activation(lam_q[:, :, :], lam_q[:, :, :], ACT.Exp)
            e.activation(lam_k[:, :, :], lam_k[:, :, :], ACT.Exp)
            e.activation(head[:, 2, :], head[:, 1, :], ACT.Exp, scale=-1.0)
            e.activation(part[:, 4, :], part[:, 0, :], ACT.Exp, scale=float(P))
            e.activation(part[:, 5, :], part[:, 2, :], ACT.Exp, scale=-1.0).then_inc(s_exp, 1)
            weight_sum(KT)
            unmagic(0)
            e.wait_ge(s_exp, 2)
            e.activation(lam_q[:, :, :], lam_q[:, :, :], ACT.Copy, scale=QL_SCALE)
            e.activation(lam_k[:, :, :], lam_k[:, :, :], ACT.Copy, scale=QKV_SCALE).then_inc(s_tab, 1)
            for c in range(1, KT):
                unmagic(c)
            e.wait_ge(s_mask, 1)
            e.activation(mask[:, :, :], mask[:, :, :], ACT.Copy, scale=SCORE_SCALE).then_inc(s_tab, 1)

            def body(blk):
                for it in SEQUENCE_0 if isinstance(blk, int) else SEQUENCE:
                    if it[0] == "WB":
                        n = it[1]
                        e.wait_ge(s_scale, n + 1)
                        last = e.activation(piece_parts(n)[0], slot(n), ACT.Copy, scale=ws[:, n:n + 1])
                        if n >= DVE_PIECES:
                            last = e.activation(slot(n), slot(n), ACT.Copy, scale=ws[:, n:n + 1])
                        last.then_inc(s_whi, 1)
                    elif it[0] == "WP":
                        unmagic(KT)
                    scalar_item(e, it, blk)

            blocks(e, body)

        @block.tensor
        def _(e):
            e.sem_inc(pe["ZT"].sem, pe["ZT"].before)
            e.wait_ge(s_ident, 2)
            for it in FIRST_TILES:
                tensor_item(e, it, -1, FIRST_TILES)
            e.wait_ge(s_sum, 1)
            e.matmul(b_gate[:, 0:1], state1[:, :], beta[:, 0:1], start=True, stop=True).then_inc(s_ones, 1)
            e.wait_ge(s_abs, KT)
            e.matmul(b_up[:, 0:1], state1[:, :], beta[:, 1:2], start=True, stop=True).then_inc(s_ones, 1)
            e.wait_ge(s_tern, KT)

            with e.Fori(0, NBLK) as blk:
                for it in SEQUENCE:
                    tensor_item(e, it, blk, SEQUENCE)

        @block.vector
        def _(e):
            done = [0]

            def link(ins):
                done[0] += 1
                ins.then_inc(s_pro, 1)
                e.wait_ge(s_pro, done[0])

            e.memset(diag[:, :], 0.0)
            link(e.memset(state1[:, :], 1.0))
            for h in range(HPG):
                r = slice(HD * h, HD * (h + 1))
                e.memset(diag[r, r], 1.0)
            for name in ("Q", "K", "KT", "KVM", "SM", "OUT", "SUM", "Z", "Y", "GT", "GL"):
                e.sem_inc(ve[name].sem, ve[name].before)
            vector_item(e, FIRST_TILES[0], -1)

            def power(a, b):
                link(e.tensor_scalar(am[:, a:b], am[:, a:b], LEAST, None, ALU.max))
                link(e.tensor_scalar(p2[:, a:b].bitcast(U32), am[:, a:b].bitcast(U32), 0x7F800000, None, ALU.bitwise_and))
                link(e.reciprocal(ip[:, a:b], p2[:, a:b]))

            e.wait_ge(ld_qn, 16)
            link(e.tensor_reduce(am[:, 12:13], qn_b[:, :], axis=AX.X, op=ALU.max, apply_absolute_value=True))
            power(12, 13)
            link(e.tensor_scalar(qn_b[:, :], qn_b[:, :], ip[:, 12:13], H_SCALE, ALU.mult, ALU.mult))
            for it in FIRST_TILES[1:]:
                vector_item(e, it, -1)
            e.wait_ge(ld_qkv[KT - 1], 16)
            link(e.tensor_reduce(beta[:, 15:16], raw(KT - 1)[0], axis=AX.X, op=ALU.add, apply_absolute_value=True))
            e.wait_ge(s_abs, KT - 1)
            e.tensor_reduce(beta[:, 0:1], beta[:, 12:16], axis=AX.X, op=ALU.add).then_inc(s_sum, 1)
            e.wait_ge(s_ones, 1)
            link(e.tensor_scalar(beta[:, 2:3], b_gate[:, 0:1], 1.0 / (3 * D * D), 1e-5, ALU.mult, ALU.max))
            link(e.reciprocal(beta[:, 4:5], beta[:, 2:3]))

            for c in range(KT):
                if c == KT - 1:
                    e.wait_ge(s_ones, 2)
                    link(e.tensor_scalar(beta[:, 3:4], b_up[:, 0:1], 1.0 / (D * D), 1e-5, ALU.mult, ALU.max))
                    link(e.reciprocal(beta[:, 5:6], beta[:, 3:4]))
                w = raw(c)[0]
                link(e.tensor_scalar(w, w, beta[:, 4:5], MAGIC, ALU.mult, ALU.add))
                e.tensor_scalar(w, w, MAGIC + 1.0, MAGIC - 1.0, ALU.min, ALU.max).then_inc(s_clip, 1)
            e.sem_inc(ve["CHAIN"].sem, ve["CHAIN"].before - chain[0])
            link(e.tensor_scalar(beta[:, 6:7], beta[:, 2:3], p2[:, 12:13], 1.0 / H_SCALE, ALU.mult, ALU.mult))
            link(e.tensor_scalar(beta[:, 7:8], beta[:, 6:7], beta[:, 6:7], OUT_UNIT * HD ** -0.5, ALU.mult, ALU.mult))
            e.wait_ge(s_exp, 2)
            e.tensor_scalar(head[:, 3, :], head[:, 2, :], beta[:, 6:7], beta[:, 7:8], ALU.mult, ALU.mult)
            e.wait_ge(s_tab, 1)

            def weights(it):
                n = it[1]
                kind, q = PIECES[n]
                if it[0] == "WN":
                    e.wait_ge(ld_on, 32)
                    link(e.tensor_reduce(am[:, 13:14], op_b[:, :], axis=AX.X, op=ALU.max, apply_absolute_value=True))
                    power(13, 14)
                    link(e.tensor_tensor(op_b[:, :], op_b[:, :], on2_b[:, :], ALU.mult))
                    e.tensor_scalar(op_b[:, :], op_b[:, :], ip[:, 13:14], H_SCALE, ALU.mult, ALU.mult)
                    e.tensor_tensor(on2_b[:, :], on2_b[:, :], on2_b[:, :], ALU.mult)
                    link(e.tensor_scalar(beta[:, 8:9], beta[:, 3:4], p2[:, 13:14], 1.0 / H_SCALE, ALU.mult, ALU.mult))
                elif it[0] == "WA":
                    e.wait_ge(ld_piece[n % 2], 16 * (n // 2 + 1))
                    e.tensor_reduce(pm[:, n:n + 1], slot(n), axis=AX.XY, op=ALU.max,
                                    apply_absolute_value=True).then_inc(s_red, 1)
                elif it[0] == "WB":
                    e.wait_ge(s_all, 16 * (n + 1))
                    link(e.tensor_reduce(am[:, n:n + 1], max_row[n], axis=AX.X, op=ALU.max))
                    power(n, n + 1)
                    if kind == "gate":
                        e.tensor_scalar(sgate[:, q:q + 1], p2[:, n:n + 1], 2.0 ** -24, None, ALU.mult)
                        e.tensor_scalar(cu[:, q:q + 1], ip[:, n:n + 1], 2.0 ** -29, None, ALU.mult)
                    if kind == "down":
                        g, u = PIECES.index(("gate", q)), PIECES.index(("up", q))
                        link(e.tensor_scalar(cd[:, q:q + 1], p2[:, g:g + 1], p2[:, u:u + 1], None, ALU.mult))
                        e.tensor_scalar(cd[:, q:q + 1], cd[:, q:q + 1], p2[:, n:n + 1], 2.0 ** -9, ALU.mult, ALU.mult)
                    e.tensor_scalar(ws[:, n:n + 1], ip[:, n:n + 1], 2.0 ** 14, None, ALU.mult).then_inc(s_scale, 1)
                elif it[0] == "WC" and n < DVE_PIECES:
                    e.wait_ge(s_scale, n + 1)
                    e.wait_ge(s_whi, n + 1)
                    hi_part, lo_part = piece_parts(n)
                    e.scalar_tensor_tensor(out=lo_part, in0=slot(n), scalar=ws[:, n:n + 1], in1=hi_part,
                                           op0=ALU.mult, op1=ALU.subtract).then_inc(cut(n)[0], 1)

            def body(blk):
                chain[0] = 0
                if not isinstance(blk, int):
                    e.wait_ge(ve["S2"].sem, ve["S2"].at(blk, 0))
                    e.tensor_scalar(state[:, 0, :, :].rearrange("p j n -> p (j n)"),
                                    state[:, 0, :, :].rearrange("p j n -> p (j n)"),
                                    keep[:, 0, bass.ds(blk, 1)], keep[:, 1, bass.ds(blk, 1)], ALU.max, ALU.min)\
                        .then_inc(ve["KEEP"].sem, 1)
                    e.wait_ge(ve["KEEP"].sem, ve["KEEP"].at(blk, 0))
                for it in SEQUENCE_0 if isinstance(blk, int) else SEQUENCE:
                    if it[0][0] == "W":
                        weights(it)
                    else:
                        vector_item(e, it, blk)
                assert chain[0] == ve["CHAIN"].per

            blocks(e, body)


def kernel(L0_attn_x, L0_attn_qkv_w, L0_attn_qkv_norm_w, L0_attn_proj_w, L0_attn_proj_norm_w,
           L0_attn_norm_w, L0_attn_s, L0_ffn_w_gate, L0_ffn_w_up, L0_ffn_w_down):
    import concourse.bacc as bacc
    from concourse.bass_utils import run_bass_kernel_spmd

    def a(t):
        return np.asarray(t)

    hidden = lambda w: a(w).T.reshape(KT, P, NQ, HID // NQ).transpose(2, 1, 0, 3)
    arrays = {
        "x": a(L0_attn_x).reshape(TOK, D),
        "qkv_t": a(L0_attn_qkv_w).T.reshape(KT, P, 3 * D).transpose(1, 0, 2).reshape(P, KT * 3 * D),
        "proj_t": a(L0_attn_proj_w).T.reshape(KT, P, D).transpose(1, 0, 2).reshape(P, KT * D),
        "gate_t": hidden(L0_ffn_w_gate),
        "up_t": hidden(L0_ffn_w_up),
        "down_t": a(L0_ffn_w_down).T.reshape(NQ, HPQ, P, D).transpose(0, 2, 1, 3),
        "qn_w": a(L0_attn_qkv_norm_w), "on_w": a(L0_attn_norm_w), "pn_w": a(L0_attn_proj_norm_w),
        "s_row": a(L0_attn_s),
        "s_part": np.repeat(a(L0_attn_s).reshape(GROUPS, HPG).T, HD, axis=0),
    }
    arrays = {n: np.ascontiguousarray(t) for n, t in arrays.items()}
    nc = bacc.Bacc("TRN2", target_bir_lowering=False, num_devices=1, dynamic_dma_scratch_size=64)
    aps = [nc.dram_tensor(n, t.shape, mybir.dt.from_np(t.dtype), kind="ExternalInput").ap() for n, t in arrays.items()]
    out = nc.dram_tensor("out", (TOK, D), F32, kind="ExternalOutput").ap()
    spill = nc.dram_tensor("spill", (len(PIECES), P), F32).ap()
    build(nc, *aps, out, spill)
    r = run_bass_kernel_spmd(nc, [arrays], core_ids=[0])
    return r.results[0]["out"].reshape(BATCH, SEQ, D)
```

```python
import numpy as np
import concourse.bass as bass
from concourse import mybir

F32, F16, U32, I32 = mybir.dt.float32, mybir.dt.float16, mybir.dt.uint32, mybir.dt.int32
ALU = mybir.AluOpType
ACT = mybir.ActivationFunctionType
AX = mybir.AxisListType

P = 128
D = 512
KT = D // P
HEADS, HD = 16, 32
HPG = P // HD
GROUPS = HEADS // HPG
BATCH, SEQ = 4, 1024
TOK = BATCH * SEQ
BLK = 512
TPB = BLK // P
BPB = SEQ // BLK
NBLK = TOK // BLK
HALF = 2 * P
HID = 2048
HT = HID // P
NQ = 4
HPQ = HT // NQ
STEPS = 2 * GROUPS
SMALL = 280

LN_EPS, RMS_EPS, OUT_EPS = 1e-5, float(np.finfo(np.float32).eps), 1e-6
MAGIC = 1.5 * 2.0 ** 23
LEAST = 1e-12
X_SCALE = 2.0 ** 10
H_SCALE = 2.0 ** 9
QKV_SCALE = 2.0 ** -4
SCORE_SCALE = 2.0 ** -20
QL_SCALE = 2.0 ** -24
OUT_UNIT = 2.0 ** 32


class Count:

    def __init__(self, nc, name, per, before=0):
        self.sem, self.per, self.before = nc.alloc_semaphore(name), per, before

    def at(self, blk, k):
        if isinstance(blk, int):
            return self.before + self.per * blk + k
        return blk * self.per + (self.before + k)


def schedule():
    tiles = [[(kind, h) for h in range(HPQ * q, HPQ * (q + 1)) for kind in ("G", "U")] for q in range(NQ)]
    down = [[("D", q, c) for c in range(TPB)] for q in range(NQ)]

    def mix(q):
        return [x for n in range(TPB) for x in (*tiles[q][2 * n:2 * n + 2], down[q - 1][n])]

    fill = iter(tiles[0] + mix(1) + mix(2) + tiles[3] + down[2] + down[3])

    attention = [("Q", 0), ("K", 0), ("V", 0), ("V", 1)]
    for s in range(STEPS):
        after = s == GROUPS
        attention += [("SC", s, 0), ("KT", s)] + [("NR", 0), ("ZT", 0)] * after
        attention += [("KV", s), ("O", s, 0), ("SC", s, 1)]
        if s + 1 < STEPS:
            attention += [("Q", s + 1), ("K", s + 1)] + [("PJ", 0)] * after
        else:
            attention += [("ST", 0)]
        attention += [("ZT", 1)] * after + [("O", s, 1)] + [("PJ", 1)] * after
        if s + 1 == GROUPS:
            attention += [("V", 2), ("NA", 0), ("V", 3), ("NA", 1)]
    attention += [("TX", 0), ("TX", 1), ("NA", 2), ("NA", 3), ("NR", 1), ("TH", 0), ("TH", 1), ("ZT", 2), ("ST", 1),
                  ("PJ", 2), ("ZT", 3), ("TX", 2), ("TX", 3), ("PJ", 3), ("TH", 2), ("TH", 3)]
    seq = []
    for n, it in enumerate(attention):
        seq += [next(fill) for _ in range(int(FILLS[n]))] + [it]
    return seq + list(fill)


def with_weights(seq):
    at = {n: [] for n in range(NQ * (2 * HPQ + TPB))}
    for piece, ns in PIECE_FILLS.items():
        load, largest, row, scale, cut_at = ns
        if load is not None:
            at[load].append(("WL", piece))
        at[largest + 1].append(("WS", piece))
        at[row].append(("WR", piece))
        at[scale].append(("WB", piece))
        for kind, n in (("WA", largest), ("WH", cut_at), ("WC", cut_at)):
            for i in range(4):
                at[n + i // 2].append((kind, piece, i))
    order = ("WL", "WA", "WS", "WR", "WB", "WH", "WC")
    quarters = lambda kind, n: [(kind, n, i) for i in range(4)]
    out, fills = [], 0
    for it in seq:
        out += {("Q", 0): quarters("WA", 0) + [("WS", 0), ("WR", 0)] + quarters("WA", 1) + [("WS", 1), ("WR", 1)],
                ("K", 0): [("WB", 0)],
                ("V", 0): [("WB", 1)] + quarters("WH", 0) + quarters("WC", 0) + [("WP", 0), ("WL", 2)]
                + quarters("WH", 1) + quarters("WC", 1),
                ("U", 1): [("WQ", 0)], ("U", 5): [("WN", 0)]}.get(it, [])
        if it[0] in ("G", "U", "D"):
            out += sorted(at[fills], key=lambda x: (x[1], order.index(x[0])))
            fills += 1
        out.append(it)
    for q in range(NQ):
        for kind, it in (("gate", ("G", HPQ * q)), ("up", ("U", HPQ * q)), ("down", ("D", q, 0))):
            assert out.index(("WC", PIECES.index((kind, q)), 3)) < out.index(it), (kind, q)
    for n in range(2, len(PIECES)):
        assert out.index(("WC", n - 2, 3)) < out.index(("WA", n, 0)), n
    return out


FILLS = "00001020001110200002102000021020000200000012000010110002000021020000210200021001100101010010"
SEQUENCE = schedule()
PIECES = [("gate", 0), ("up", 0), ("gate", 1), ("up", 1), ("down", 0), ("gate", 2), ("up", 2), ("down", 1),
          ("gate", 3), ("up", 3), ("down", 2), ("down", 3)]
PIECE_FILLS = {2: (None, 1, 2, 3, 3), 3: (1, 2, 4, 5, 5), 4: (5, 6, 8, 9, 9),
               5: (7, 9, 11, 12, 12), 6: (11, 13, 15, 16, 16), 7: (15, 16, 18, 18, 19),
               8: (19, 22, 24, 25, 25), 9: (23, 26, 28, 29, 30), 10: (28, 30, 32, 33, 33),
               11: (31, 34, 36, 37, 37)}
SEQUENCE_0 = with_weights(SEQUENCE)
FIRST_TILES = [("ST", 0), ("TX", 0), ("TX", 1), ("TH", 0), ("TH", 1),
               ("ST", 1), ("TX", 2), ("TX", 3), ("TH", 2), ("TH", 3)]
POOL_TERNARY = 3
DVE_PIECES = 2
Y_ADDS = [it for it in SEQUENCE if it[0] in ("D", "PJ")]
POOLED = [it for it in SEQUENCE if it[0] in ("V", "Q", "K", "KT", "KV", "ZT", "PJ", "TX", "TH", "D")]
N_SHARED = 4
assert len(POOLED) % N_SHARED == 0


def build(nc, x, qkv_t, proj_t, gate_t, up_t, down_t, qn_w, on_w, pn_w, s_row, s_part, out, spill):
    def sb(name, shape, dt):
        return nc.alloc_sbuf_tensor(name, shape, dt)

    wg = [sb(f"wg_{n}", [P, KT, HID], F16) for n in ("hi", "lo")]
    wu = [sb(f"wu_{n}", [P, KT, HID], F16) for n in ("hi", "lo")]
    wd = [sb(f"wd_{n}", [P, HT, D], F16) for n in ("hi", "lo")]
    wq = sb("wq", [P, KT, 3 * D], F16)
    wp = sb("wp", [P, KT, D], F16)
    stage = sb("stage", [P, 2, 4, 512], F32)
    arena = sb("arena", [P, 8192], F32)
    gated = [[arena[:, 2048 * b + 1024 * n:2048 * b + 1024 * (n + 1)].bitcast(F16)
              .rearrange("p (t n) -> p t n", t=HPQ) for n in range(2)] for b in range(2)]
    y = arena[:, 4096:6144].rearrange("p (c n) -> p c n", c=TPB)
    o = arena[:, 6144:7168].rearrange("p (c n) -> p c n", c=2)
    osq = arena[:, 7168:7680]
    z = [arena[:, 7680 + 256 * n:7936 + 256 * n].bitcast(F16).rearrange("p (k t) -> p k t", k=KT)
         for n in range(2)]
    xt = [sb(f"xt_{n}", [P, KT, BLK], F16) for n in ("hi", "lo")]
    ht = [sb(f"ht_{n}", [P, KT, BLK], F16) for n in ("hi", "lo")]
    xin = sb("xin", [P, 2, D], F32)
    v = [sb(f"v_{n}", [P, 2, D], F16) for n in ("hi", "lo")]
    q_parts = sb("q_parts", [P, 2, HALF], F16)
    k_parts = sb("k_parts", [P, 2, HALF], F16)
    q_stack, k_stack = (sb(n, [3 * HD, HPG, HALF], F16) for n in ("q_stack", "k_stack"))
    ql = sb("ql", [P, 2, HALF], F32)
    kl = sb("kl", [P, HALF], F32)
    kt = [k_parts[:, n, :] for n in range(2)]
    kvm = kl[:, :].rearrange("p (c t) -> p c t", c=2)
    state = sb("state", [P, 2, GROUPS, P], F32)
    state1 = sb("state1", [P, P], F32)
    sm = sb("sm", [P, HPG, P], F32)
    smp = [sb(f"sm_{n}", [P, HPG, P], F16) for n in ("hi", "lo")]
    sg = sb("sg", [P, BLK], F32)
    ramp_diff, ramp, ramp_back = sm[:, 2, :], sm[:, 3, :], sg[:, 0:P]
    x_late = wd[0][:, 3 * HPQ:4 * HPQ, :].rearrange("p i n -> p (i n)").bitcast(F32).rearrange("p (c n) -> p c n", c=2)
    max_row = [x_late[:, n % 8 // 4, P * (n % 4):P * (n % 4 + 1)] for n in range(len(PIECES))]
    mask = sb("mask", [P, HEADS, P], F32)
    lam_q = sb("lam_q", [P, GROUPS, P], F32)
    lam_k = sb("lam_k", [P, GROUPS, P], F32)
    diag = sb("diag", [P, P], F32)
    qn_b = sb("qn_b", [P, D], F32)
    on2_b = sb("on2_b", [P, D], F32)
    op_b = sb("op_b", [P, D], F32)
    ident = sb("ident", [P, P], F32)
    small, used = sb("small", [P, SMALL], F32), [0]

    def table(*shape):
        start = used[0]
        used[0] += int(np.prod(shape))
        assert used[0] <= SMALL
        flat = small[:, start:used[0]]
        return flat if len(shape) == 1 else flat.rearrange("p (a b) -> p a b", a=shape[0])

    sr = table(HEADS)
    sp = table(GROUPS)
    head = table(4, HEADS)
    part = table(6, GROUPS)
    pm = table(16)
    pm4 = table(4)
    am = table(16)
    p2 = table(16)
    ip = table(16)
    ws = table(16)
    sgate = table(NQ)
    cu = table(NQ)
    cd = table(NQ)
    keep = table(2, NBLK)
    beta = table(16)
    st6 = table(2, 6)
    idle = table(1)
    mv = table(2, 2)
    var_ab = table(3, 2)
    rs = table(2, 2)
    mhalf = table(4)
    nrm = table(5, 2)

    banks = [nc.alloc_psum_tensor(f"bank{n}", [P, 512], F32) for n in range(8)]
    b_gate, b_up, b_sc, b_o = banks[0], banks[1], banks[2], banks[3]
    shared = banks[4:8]

    def bank_of(it):
        return shared[POOLED.index(it) % N_SHARED]

    C = lambda name, per, before=0: Count(nc, name, per, before)
    pe = {k: C("pe_" + k, n, b) for k, n, b in (
        ("V", 4, 0), ("Q", 8, 0), ("K", 8, 0), ("KT", 8, 0), ("KV", 8, 0), ("SC", 16, 0), ("O", 16, 0),
        ("ZT", 4, 1), ("PJ", 4, 0), ("TX", 4, 4), ("TH", 4, 4), ("G", 16, 0), ("U", 16, 0), ("D", 16, 0))}
    ac = {k: C("act_" + k, n, b) for k, n, b in (
        ("V", 4, 0), ("Q", 16, 0), ("K", 16, 0), ("KT", 8, 0), ("SM", 16, 0), ("SQ", 4, 0), ("Z", 4, 0),
        ("TX", 4, 4), ("TH", 4, 4), ("SILU", 16, 1), ("GH", 16, 0))}
    ve = {k: C("dve_" + k, n, b) for k, n, b in (
        ("V", 4, 0), ("Q", 8, 1), ("K", 8, 1), ("KT", 8, 1), ("KVM", 8, 1), ("S1", 8, 0), ("S2", 8, 0),
        ("SM", 16, 1), ("SL", 16, 0), ("OUT", 8, 1), ("SUM", 4, 1), ("U", 2, 0), ("ZN", 4, 0), ("Z", 4, 1),
        ("Y", 20, 21), ("XN", 4, 4), ("H", 4, 4), ("TX", 4, 4), ("TH", 4, 4), ("VAR", 2, 2),
        ("GT", 16, 1), ("GL", 16, 1), ("CHAIN", 28, 28), ("KEEP", 1, 0))}
    po = {k: C("pool_" + k, n, b) for k, n, b in (("RS", 2, 2), ("R", 2, 0))}
    ld_x = [C(f"ld_x{n}", 32) for n in range(2)]
    ld_y, st_y = C("ld_y", 16), C("st_y", 64, 16)

    def sem(name):
        return nc.alloc_semaphore(name)

    ld_qn, ld_on, ld_first = sem("ld_qn"), sem("ld_on"), [sem(f"ld_first{c}") for c in range(TPB)]
    ld_tab, ld_proj = sem("ld_tab"), sem("ld_proj")
    ld_qkv = [sem(f"ld_qkv{n}") for n in range(KT)]
    ld_piece = [sem(f"ld_piece{n}") for n in range(2)]
    s_ident, s_pool, s_arg, s_exp, s_mask, s_tab = (sem(n) for n in (
        "ident", "pool_chain", "exponents", "exp", "masked", "tables"))
    s_pro, s_sum, s_tern, s_red, s_scale, s_whi, s_ones, s_abs, s_clip, s_spill = (sem(n) for n in (
        "pro_chain", "beta_sum", "ternary", "piece_max", "piece_scale", "piece_hi",
        "beta_total", "beta_part", "clipped", "max_spilled"))
    s_inverse, s_clip_pool = sem("beta_inverse"), sem("clipped_pool")
    s_all = [sem(f"piece_allmax{n}") for n in range(2)]
    s_wlo = {"dve": sem("piece_lo_dve"), "pool": sem("piece_lo_pool")}

    dram = {"gate": gate_t, "up": up_t, "down": down_t}

    def slot(n):
        return stage[:, n % 2, :, :]

    def piece_parts(n):
        kind, q = PIECES[n]
        if kind == "down":
            return [w[:, HPQ * q:HPQ * (q + 1), :] for w in wd]
        return [w[:, :, 512 * q:512 * (q + 1)] for w in (wg if kind == "gate" else wu)]

    def cut(n):
        return (s_wlo["dve"], n + 1) if n < DVE_PIECES else (s_wlo["pool"], n + 1 - DVE_PIECES)

    def raw(c):
        if c < KT:
            return arena[:, 3 * D * c:3 * D * (c + 1)], wq[:, c, :]
        return arena[:, 6144:8192], wp[:, :, :].rearrange("p k n -> p (k n)")

    def x_tile(blk, c):
        return x_late[:, c % 2, :] if ahead(blk) and c >= 2 else xin[:, c % 2, :]

    def ahead(blk):
        return isinstance(blk, int) and blk < 0

    def shared_free(it, blk, executed):
        order = [i for i in POOLED if i in executed]
        n, at = order.index(it), bank_of(it)
        for back in range(1, len(order) + 1):
            other = order[n - back]
            if bank_of(other) is at:
                wrapped = n - back < 0
                break
        if wrapped and ahead(blk):
            return None
        cnt, k = {"D": lambda: (ve["Y"], Y_ADDS.index(other) + 1), "PJ": lambda: (ve["Y"], Y_ADDS.index(other) + 1),
                  "ZT": lambda: (ve["Z"], other[1] + 1), "KV": lambda: (ve["KVM"], other[1] + 1),
                  }.get(other[0], lambda: (ve[other[0]], other[1] + 1))()
        return cnt.sem, cnt.at(blk, k - (cnt.per if wrapped else 0))

    def tensor_item(e, it, blk, executed):
        kind = it[0]
        if kind in ("V", "Q", "K", "KT", "KV", "ZT", "PJ", "TX", "TH", "D"):
            free = shared_free(it, blk, executed)
            if free:
                e.wait_ge(*free)
            bank = bank_of(it)

        def products(dst, lhs, rhs, start=True, stop=True):
            for n, (a, b) in enumerate(zip(lhs, rhs)):
                last = e.matmul(dst, a, b, start=start and n == 0, stop=stop and n == len(lhs) - 1)
            return last

        if kind == "V":
            c = it[1]
            e.wait_ge(ve["TH"].sem, ve["TH"].at(blk, c + 1 - 4))
            t = slice(P * c, P * (c + 1))
            products(bank[:, :], [ht[n][:, k, t] for k in range(KT) for n in range(2)],
                     [wq[:, k, 2 * D:3 * D] for k in range(KT) for n in range(2)]).then_inc(pe["V"].sem, 1)
        elif kind in ("Q", "K"):
            s = it[1]
            a, j = divmod(s, GROUPS)
            e.wait_ge(ve["TH"].sem, ve["TH"].at(blk, 2 * a + 2 - 4))
            f = (D if kind == "K" else 0) + P * j
            products(bank[:, 0:HALF], [wq[:, k, f:f + P] for k in range(KT) for n in range(2)],
                     [ht[n][:, k, HALF * a:HALF * (a + 1)] for k in range(KT) for n in range(2)])\
                .then_inc(pe[kind].sem, 1)
        elif kind == "KT":
            s = it[1]
            e.wait_ge(ve["K"].sem, ve["K"].at(blk, s + 1))
            for c in range(2):
                last = e.transpose(bank[:, P * c:P * (c + 1)], kl[:, P * c:P * (c + 1)], ident[:, :])
            last.then_inc(pe["KT"].sem, 1)
        elif kind == "SC":
            _, s, c = it
            e.wait_ge(ve["K"].sem, ve["K"].at(blk, s + 1))
            e.wait_ge(ac["K"].sem, ac["K"].at(blk, 2 * (s + 1)))
            e.wait_ge(ve["SM"].sem, ve["SM"].at(blk, 2 * s + c))
            t = slice(P * c, P * (c + 1))
            for h in range(HPG):
                last = e.matmul(b_sc[:, P * h:P * (h + 1)], k_stack[:, h, t], q_stack[:, h, t], start=True, stop=True)
            last.then_inc(pe["SC"].sem, 1)
        elif kind == "KV":
            s = it[1]
            j = s % GROUPS
            e.wait_ge(ve["KT"].sem, ve["KT"].at(blk, s + 1))
            e.wait_ge(ve["V"].sem, ve["V"].at(blk, 2 * (s // GROUPS) + 2))
            for c in range(2):
                t, f = slice(P * c, P * (c + 1)), slice(P * j, P * (j + 1))
                last = products(bank[:, t], [kt[0][:, t], kt[0][:, t], kt[1][:, t]],
                                [v[n][:, c, f] for n in (0, 1, 0)])
            last.then_inc(pe["KV"].sem, 1)
        elif kind == "O":
            _, s, c = it
            a, j = divmod(s, GROUPS)
            e.wait_ge(ve["SL"].sem, ve["SL"].at(blk, 2 * s + c + 1))
            if c == 0:
                e.wait_ge(ve["OUT"].sem, ve["OUT"].at(blk, s))
                cross = state[:, a, j, :]
            else:
                e.wait_ge(ve["S1"].sem, ve["S1"].at(blk, s + 1))
                cross = state1[:, :]
            products(b_o[:, P * c:P * (c + 1)], [ql[:, s % 2, P * c:P * (c + 1)]], [cross], stop=False)
            for h in range(HPG):
                f = slice(P * j + HD * h, P * j + HD * (h + 1))
                last = products(b_o[:, P * c + HD * h:P * c + HD * (h + 1)],
                                [smp[0][:, h, :], smp[0][:, h, :], smp[1][:, h, :]],
                                [v[n][:, c, f] for n in (0, 1, 0)], start=False, stop=h == HPG - 1)
            last.then_inc(pe["O"].sem, 1)
        elif kind == "ZT":
            c = it[1]
            e.wait_ge(ve["ZN"].sem, ve["ZN"].at(blk, c + 1))
            for k in range(KT):
                last = e.transpose(bank[:, P * k:P * (k + 1)], o[:, c % 2, P * k:P * (k + 1)], ident[:, :])
            last.then_inc(pe["ZT"].sem, 1)
        elif kind == "PJ":
            c = it[1]
            if c == 0:
                e.wait_ge(s_tern, KT + 1)
            e.wait_ge(ve["Z"].sem, ve["Z"].at(blk, c + 1))
            products(bank[:, :], [z[n][:, k, :] for k in range(KT) for n in range(2)],
                     [wp[:, k, :] for k in range(KT) for n in range(2)]).then_inc(pe["PJ"].sem, 1)
        elif kind in ("TX", "TH"):
            c = it[1]
            made = ve["XN" if kind == "TX" else "H"]
            e.wait_ge(made.sem, made.at(blk, c + 1))
            for k in range(KT):
                last = e.transpose(bank[:, P * k:P * (k + 1)], x_tile(blk, c)[:, P * k:P * (k + 1)], ident[:, :])
            last.then_inc(pe[kind].sem, 1)
        elif kind in ("G", "U"):
            h = it[1]
            if (kind, h) == ("G", 0):
                e.wait_ge(ve["TX"].sem, ve["TX"].at(blk, 0))
            if h % HPQ == 0:
                e.wait_ge(*cut(PIECES.index(("gate" if kind == "G" else "up", h // HPQ))))
            t = slice(P * h, P * (h + 1))
            w, bank, free = (wg, b_gate, ac["SILU"]) if kind == "G" else (wu, b_up, ve["GT"])
            e.wait_ge(free.sem, free.at(blk, h))
            products(bank[:, :], [w[n][:, k, t] for k in range(KT) for n in (0, 0, 1)],
                     [xt[n][:, k, :] for k in range(KT) for n in (0, 1, 0)]).then_inc(pe[kind].sem, 1)
        elif kind == "D":
            _, q, c = it
            e.wait_ge(ve["GL"].sem, ve["GL"].at(blk, HPQ * (q + 1)))
            if c == 0:
                e.wait_ge(*cut(PIECES.index(("down", q))))
            g, t = gated[q % 2], slice(P * c, P * (c + 1))
            products(bank[:, :], [g[n][:, i, t] for i in range(HPQ) for n in (0, 0, 1)],
                     [wd[n][:, HPQ * q + i, :] for i in range(HPQ) for n in (0, 1, 0)]).then_inc(pe["D"].sem, 1)

    def scalar_item(e, it, blk):
        kind = it[0]
        if kind == "V":
            e.wait_ge(pe["V"].sem, pe["V"].at(blk, it[1] + 1))
            e.activation(v[0][:, it[1] % 2, :], bank_of(it)[:, :], ACT.Copy, scale=QKV_SCALE).then_inc(ac["V"].sem, 1)
        elif kind in ("Q", "K"):
            parts = q_parts if kind == "Q" else k_parts
            e.wait_ge(pe[kind].sem, pe[kind].at(blk, it[1] + 1))
            e.activation(parts[:, 0, :], bank_of(it)[:, 0:HALF], ACT.Copy, scale=QKV_SCALE).then_inc(ac[kind].sem, 1)
            stack, at = (q_stack, (0, 2)) if kind == "Q" else (k_stack, (0, 1))
            e.wait_ge(ac[kind].sem, ac[kind].at(blk, 2 * it[1] + 1))
            for h in range(HPG):
                for g in at:
                    last = e.activation(stack[HD * g:HD * (g + 1), h, :], parts[HD * h:HD * (h + 1), 0, :], ACT.Copy)
            last.then_inc(ac[kind].sem, 1)
        elif kind == "KT":
            e.wait_ge(pe["KT"].sem, pe["KT"].at(blk, it[1] + 1))
            e.activation(kt[0], bank_of(it)[:, 0:HALF], ACT.Copy).then_inc(ac["KT"].sem, 1)
        elif kind == "SC":
            _, s, c = it
            e.wait_ge(ve["SM"].sem, ve["SM"].at(blk, 2 * s + c + 1))
            e.activation(smp[0][:, :, :], sm[:, :, :], ACT.Copy).then_inc(ac["SM"].sem, 1)
        elif kind == "NA":
            c = it[1]
            e.wait_ge(ve["OUT"].sem, ve["OUT"].at(blk, 4 * (c // 2) + 4))
            e.wait_ge(ve["SUM"].sem, ve["SUM"].at(blk, c))
            e.activation(osq[:, :], o[:, c % 2, :], ACT.Square, accum_out=nrm[:, 0, c % 2:c % 2 + 1])\
                .then_inc(ac["SQ"].sem, 1)
        elif kind == "ZT":
            c = it[1]
            e.wait_ge(pe["ZT"].sem, pe["ZT"].at(blk, c + 1))
            e.activation(z[0][:, :, :], bank_of(it)[:, :].rearrange("p (k t) -> p k t", k=KT), ACT.Copy)\
                .then_inc(ac["Z"].sem, 1)
        elif kind in ("TX", "TH"):
            c = it[1]
            dst, scale = (xt, X_SCALE) if kind == "TX" else (ht, 1.0)
            e.wait_ge(pe[kind].sem, pe[kind].at(blk, c + 1))
            e.activation(dst[0][:, :, P * c:P * (c + 1)], bank_of(it)[:, :].rearrange("p (k t) -> p k t", k=KT),
                         ACT.Copy, scale=scale).then_inc(ac[kind].sem, 1)
        elif kind == "G":
            h = it[1]
            q = h // HPQ
            e.wait_ge(pe["G"].sem, pe["G"].at(blk, h + 1))
            e.wait_ge(ve["GL"].sem, ve["GL"].at(blk, h))
            e.activation(sg[:, :], b_gate[:, :], ACT.Silu, scale=sgate[:, q:q + 1]).then_inc(ac["SILU"].sem, 1)
        elif kind == "U":
            h = it[1]
            q = h // HPQ
            e.wait_ge(ve["GT"].sem, ve["GT"].at(blk, h + 1))
            e.activation(gated[q % 2][0][:, h % HPQ, :], sg[:, :], ACT.Copy).then_inc(ac["GH"].sem, 1)

    chain = [0]

    def vector_item(e, it, blk):
        kind = it[0]

        def lo(dst, src, scale, hi, ready, k):
            e.wait_ge(ready.sem, ready.at(blk, k))
            if scale == 1.0:
                return e.tensor_tensor(dst, src, hi, ALU.subtract)
            return e.scalar_tensor_tensor(out=dst, in0=src, scalar=scale, in1=hi, op0=ALU.mult, op1=ALU.subtract)

        def link(ins):
            chain[0] += 1
            ins.then_inc(ve["CHAIN"].sem, 1)
            e.wait_ge(ve["CHAIN"].sem, ve["CHAIN"].at(blk, chain[0]))

        if kind == "V":
            c = it[1] % 2
            lo(v[1][:, c, :], bank_of(it)[:, :], QKV_SCALE, v[0][:, c, :], ac["V"], it[1] + 1).then_inc(ve["V"].sem, 1)
        elif kind == "Q":
            s = it[1]
            b = bank_of(it)
            link(lo(q_parts[:, 1, :], b[:, 0:HALF], QKV_SCALE, q_parts[:, 0, :], ac["Q"], 2 * s + 1))
            for h in range(HPG):
                e.tensor_copy(q_stack[HD:2 * HD, h, :], q_parts[HD * h:HD * (h + 1), 1, :])
            e.tensor_tensor(ql[:, s % 2, :].rearrange("p (c t) -> p c t", c=2),
                            b[:, 0:HALF].rearrange("p (c t) -> p c t", c=2),
                            lam_q[:, s % GROUPS, :].unsqueeze(1).to_broadcast([P, 2, P]), ALU.mult)\
                .then_inc(ve["Q"].sem, 1)
        elif kind == "K":
            s = it[1]
            b = bank_of(it)
            link(lo(k_parts[:, 1, :], b[:, 0:HALF], QKV_SCALE, k_parts[:, 0, :], ac["K"], 2 * s + 1))
            for h in range(HPG):
                e.tensor_copy(k_stack[2 * HD:3 * HD, h, :], k_parts[HD * h:HD * (h + 1), 1, :])
            e.tensor_tensor(kl[:, :].rearrange("p (c t) -> p c t", c=2),
                            b[:, 0:HALF].rearrange("p (c t) -> p c t", c=2),
                            lam_k[:, s % GROUPS, :].unsqueeze(1).to_broadcast([P, 2, P]), ALU.mult)\
                .then_inc(ve["K"].sem, 1)
        elif kind == "KT":
            s = it[1]
            lo(kt[1], bank_of(it)[:, 0:HALF], 1.0, kt[0], ac["KT"], s + 1).then_inc(ve["KT"].sem, 1)
        elif kind == "SC":
            _, s, c = it
            j, k = s % GROUPS, 2 * s + c + 1
            e.wait_ge(pe["SC"].sem, pe["SC"].at(blk, k))
            e.tensor_tensor(sm[:, :, :], b_sc[:, :].rearrange("p (h t) -> p h t", h=HPG),
                            mask[:, HPG * j:HPG * (j + 1), :], ALU.mult).then_inc(ve["SM"].sem, 1)
            lo(smp[1][:, :, :], sm[:, :, :], 1.0, smp[0][:, :, :], ac["SM"], k).then_inc(ve["SL"].sem, 1)
        elif kind == "KV":
            s = it[1]
            a, j = divmod(s, GROUPS)
            e.wait_ge(pe["KV"].sem, pe["KV"].at(blk, s + 1))
            e.scalar_tensor_tensor(out=kvm, in0=bank_of(it)[:, 0:HALF].rearrange("p (c t) -> p c t", c=2),
                                   scalar=part[:, 5, j:j + 1], in1=diag[:, :].unsqueeze(1).to_broadcast([P, 2, P]),
                                   op0=ALU.mult, op1=ALU.mult).then_inc(ve["KVM"].sem, 1)
            e.wait_ge(ve["KVM"].sem, ve["KVM"].at(blk, s + 1))
            e.scalar_tensor_tensor(out=state1[:, :], in0=state[:, a, j, :], scalar=part[:, 4, j:j + 1],
                                   in1=kvm[:, 0, :], op0=ALU.mult, op1=ALU.add).then_inc(ve["S1"].sem, 1)
            e.wait_ge(ve["S1"].sem, ve["S1"].at(blk, s + 1))
            e.scalar_tensor_tensor(out=state[:, 1 - a, j, :], in0=state1[:, :], scalar=part[:, 4, j:j + 1],
                                   in1=kvm[:, 1, :], op0=ALU.mult, op1=ALU.add).then_inc(ve["S2"].sem, 1)
        elif kind == "O":
            _, s, c = it
            if c == 0:
                return
            a, j = divmod(s, GROUPS)
            e.wait_ge(pe["O"].sem, pe["O"].at(blk, 2 * s + 2))
            e.wait_ge(pe["ZT"].sem, pe["ZT"].at(blk, 2 * a))
            e.tensor_tensor(o[:, :, P * j:P * (j + 1)].rearrange("p c (h d) -> p c h d", h=HPG),
                            b_o[:, 0:HALF].rearrange("p (c h d) -> p c h d", c=2, h=HPG),
                            head[:, 3, HPG * j:HPG * (j + 1)].unsqueeze(1).unsqueeze(3).to_broadcast([P, 2, HPG, HD]),
                            ALU.mult).then_inc(ve["OUT"].sem, 1)
        elif kind == "NA":
            c = it[1]
            e.wait_ge(ac["SQ"].sem, ac["SQ"].at(blk, c + 1))
            e.tensor_tensor_reduce(out=osq[:, :], in0=osq[:, :], in1=on2_b[:, :], scale=1.0, scalar=0.0,
                                   op0=ALU.mult, op1=ALU.add, accum_out=nrm[:, 1, c % 2:c % 2 + 1])\
                .then_inc(ve["SUM"].sem, 1)
        elif kind == "NR":
            a = it[1]
            e.wait_ge(ve["SUM"].sem, ve["SUM"].at(blk, 2 * a + 2))
            link(e.tensor_scalar(nrm[:, 2, :], nrm[:, 0, :], RMS_EPS / D, RMS_EPS * OUT_EPS, ALU.mult, ALU.add))
            e.scalar_tensor_tensor(out=nrm[:, 3, :], in0=nrm[:, 1, :], scalar=1.0 / D, in1=nrm[:, 2, :],
                                   op0=ALU.mult, op1=ALU.add).then_inc(ve["U"].sem, 1)
            e.wait_ge(po["R"].sem, po["R"].at(blk, a + 1))
            for c in range(2):
                e.scalar_tensor_tensor(out=o[:, c, :], in0=o[:, c, :], scalar=nrm[:, 4, c:c + 1], in1=op_b[:, :],
                                       op0=ALU.mult, op1=ALU.mult).then_inc(ve["ZN"].sem, 1)
        elif kind == "ZT":
            c = it[1]
            lo(z[1][:, :, :], bank_of(it)[:, :].rearrange("p (k t) -> p k t", k=KT), 1.0, z[0][:, :, :],
               ac["Z"], c + 1).then_inc(ve["Z"].sem, 1)
        elif kind in ("PJ", "D"):
            c, k = it[-1], Y_ADDS.index(it)
            if all(i[-1] != c for i in Y_ADDS[:k]):
                e.wait_ge(ld_y.sem, ld_y.at(blk, 16))
            mine, n = (pe["PJ"], c + 1) if kind == "PJ" else (pe["D"], TPB * it[1] + c + 1)
            e.wait_ge(mine.sem, mine.at(blk, n))
            e.wait_ge(ve["Y"].sem, ve["Y"].at(blk, k))
            e.scalar_tensor_tensor(out=y[:, c, :], in0=bank_of(it)[:, :],
                                   scalar=beta[:, 8:9] if kind == "PJ" else cd[:, it[1]:it[1] + 1],
                                   in1=y[:, c, :], op0=ALU.mult, op1=ALU.add).then_inc(ve["Y"].sem, 1)
        elif kind == "ST":
            p = it[1]
            for c in range(2):
                if ahead(blk):
                    e.wait_ge(ld_first[2 * p + c], 16)
                else:
                    e.wait_ge(ld_x[c].sem, ld_x[c].at(blk, 16 * (p + 1)))
                last = e.bn_stats(st6[:, c, :], x_tile(blk, 2 * p + c))
            link(last)
            e.memset(idle[:, :], 0.0)
            for c in range(2):
                last = e.bn_aggr(mv[:, c, :], st6[:, c, :])
            link(last)
            link(e.tensor_scalar(var_ab[:, 0, :], mv[:, :, 1], LN_EPS, None, ALU.add))
            link(e.reciprocal(var_ab[:, 2, :], var_ab[:, 0, :]))
            link(e.tensor_tensor(var_ab[:, 2, :], var_ab[:, 2, :], mv[:, :, 1], ALU.mult))
            e.tensor_scalar(var_ab[:, 1, :], var_ab[:, 2, :], RMS_EPS, None, ALU.add).then_inc(ve["VAR"].sem, 1)
            e.wait_ge(po["RS"].sem, po["RS"].at(blk, p + 1))
            for c in range(2):
                t = x_tile(blk, 2 * p + c)
                e.tensor_scalar(t, t, mv[:, c, 0:1], rs[:, 0, c:c + 1],
                                ALU.subtract, ALU.mult).then_inc(ve["XN"].sem, 1)
        elif kind == "TX":
            c = it[1]
            lo(xt[1][:, :, P * c:P * (c + 1)], bank_of(it)[:, :].rearrange("p (k t) -> p k t", k=KT), X_SCALE,
               xt[0][:, :, P * c:P * (c + 1)], ac["TX"], c + 1).then_inc(ve["TX"].sem, 1)
            t = x_tile(blk, c)
            e.scalar_tensor_tensor(out=t, in0=t, scalar=rs[:, 1, c % 2:c % 2 + 1],
                                   in1=qn_b[:, :], op0=ALU.mult, op1=ALU.mult).then_inc(ve["H"].sem, 1)
        elif kind == "TH":
            c = it[1]
            lo(ht[1][:, :, P * c:P * (c + 1)], bank_of(it)[:, :].rearrange("p (k t) -> p k t", k=KT), 1.0,
               ht[0][:, :, P * c:P * (c + 1)], ac["TH"], c + 1).then_inc(ve["TH"].sem, 1)
        elif kind == "U":
            h = it[1]
            q = h // HPQ
            e.wait_ge(pe["U"].sem, pe["U"].at(blk, h + 1))
            e.wait_ge(ac["SILU"].sem, ac["SILU"].at(blk, h + 1))
            e.scalar_tensor_tensor(out=sg[:, :], in0=b_up[:, :], scalar=cu[:, q:q + 1], in1=sg[:, :],
                                   op0=ALU.mult, op1=ALU.mult).then_inc(ve["GT"].sem, 1)
            lo(gated[q % 2][1][:, h % HPQ, :], sg[:, :], 1.0, gated[q % 2][0][:, h % HPQ, :], ac["GH"], h + 1)\
                .then_inc(ve["GL"].sem, 1)

    def pool_item(e, it, blk):
        if it[0] == "ST":
            e.wait_ge(ve["VAR"].sem, ve["VAR"].at(blk, it[1] + 1))
            e.tensor_tensor(rs[:, :, :], var_ab[:, 0:2, :], mhalf[:, :].rearrange("p (a b) -> p a b", a=2), ALU.pow)\
                .then_inc(po["RS"].sem, 1)
        elif it[0] == "NR":
            e.wait_ge(ve["U"].sem, ve["U"].at(blk, it[1] + 1))
            e.tensor_tensor(nrm[:, 4, :], nrm[:, 3, :], mhalf[:, 0:2], ALU.pow).then_inc(po["R"].sem, 1)

    def rows(start, n):
        return slice(start, start + n) if isinstance(start, int) else bass.ds(start, n)

    def load_x(e, blk, row, c):
        if ahead(blk):
            e.dma_start(x_tile(blk, c), x[rows(row + P * c, P), :]).then_inc(ld_first[c], 16)
            return
        e.wait_ge(pe["TH"].sem, pe["TH"].at(blk, c - 1))
        e.dma_start(xin[:, c % 2, :], x[rows(row + P * c, P), :]).then_inc(ld_x[c % 2].sem, 16)

    def blocks(e, body):
        body(0)
        with e.Fori(1, NBLK) as blk:
            body(blk)

    with nc.Block() as block:
        @block.sync
        def _(e):
            e.sem_inc(st_y.sem, st_y.before)
            for c in range(TPB):
                load_x(e, -1, 0, c)
            e.dma_start(qn_b[:, :], qn_w.partition_broadcast(P)).then_inc(ld_qn, 16)
            for c in range(KT):
                e.dma_start(raw(c)[0], qkv_t[:, 1536 * c:1536 * (c + 1)]).then_inc(ld_qkv[c], 16)

            def load_piece(n):
                kind, q = PIECES[n]
                if n >= 2:
                    e.wait_ge(*cut(n - 2))
                e.dma_start(slot(n), dram[kind][q, :, :, :]).then_inc(ld_piece[n % 2], 16)

            e.dma_start(raw(KT)[0], proj_t).then_inc(ld_proj, 16)
            for n in range(2):
                load_piece(n)
            e.dma_start(on2_b[:, :], on_w.partition_broadcast(P)).then_inc(ld_on, 16)
            e.dma_start(op_b[:, :], pn_w.partition_broadcast(P)).then_inc(ld_on, 16)

            def body(blk):
                row = (blk + 1) % NBLK * BLK
                for it in SEQUENCE_0 if isinstance(blk, int) else SEQUENCE:
                    if it == ("V", 0):
                        if isinstance(blk, int):
                            e.wait_ge(s_tern, KT)
                        e.wait_ge(st_y.sem, st_y.at(blk, 0))
                        e.dma_start(y[:, :, :], x[rows(blk * BLK, BLK), :].rearrange("(c p) n -> p c n", p=P))\
                            .then_inc(ld_y.sem, 16)
                        for c in range(2):
                            load_x(e, blk, row, c)
                    kind, n = it[:2]
                    if kind == "TH" and n < 2:
                        load_x(e, blk, row, n + 2)
                    elif it in Y_ADDS and all(i[-1] != it[-1] for i in Y_ADDS[Y_ADDS.index(it) + 1:]):
                        c = it[-1]
                        e.wait_ge(ve["Y"].sem, ve["Y"].at(blk, Y_ADDS.index(it) + 1))
                        e.dma_start(out[rows(blk * BLK + P * c, P), :], y[:, c, :]).then_inc(st_y.sem, 16)
                    elif kind == "WL":
                        load_piece(n)
                    elif kind == "WS":
                        e.wait_ge(s_red, n + 1)
                        e.dma_start(spill[n, :], pm[:, n]).then_inc(s_spill, 16)
                    elif kind == "WR":
                        e.wait_ge(s_spill, 16 * (n + 1))
                        e.dma_start(max_row[n], spill[n, :].partition_broadcast(P)).then_inc(s_all[n % 2], 16)

            blocks(e, body)
            e.wait_ge(st_y.sem, st_y.at(NBLK, 0))

        @block.gpsimd
        def _(e):
            done = [0]

            def link(ins):
                done[0] += 1
                ins.then_inc(s_pool, 1)
                e.wait_ge(s_pool, done[0])

            e.memset(ident[:, :], 0.0).then_inc(s_ident, 1)
            e.wait_ge(s_ident, 1)
            e.affine_select(out=ident[:, :], in_=ident[:, :], compare_op=ALU.not_equal, fill=1.0, base=0,
                            pattern=[[-1, P]], channel_multiplier=1).then_inc(s_ident, 1)
            e.memset(mhalf[:, :], -0.5)
            e.iota(sm[:, 0, :].bitcast(I32), [[1, P]], base=0, channel_multiplier=-1)
            link(e.iota(sm[:, 1, :].bitcast(I32), [[1, P]], base=0, channel_multiplier=0))
            e.tensor_scalar(ramp_diff, sm[:, 0, :].bitcast(I32), 0.0, None, ALU.max)
            e.tensor_scalar(ramp_back, sm[:, 1, :].bitcast(I32), -1.0, float(P), ALU.mult, ALU.add)
            e.tensor_copy(ramp, sm[:, 1, :].bitcast(I32))
            e.wait_ge(ld_tab, 32)
            e.tensor_scalar(head[:, 0, :], sr[:, :], -1.0, None, ALU.mult)
            e.tensor_scalar(part[:, 0, :], sp[:, :], -1.0, None, ALU.mult)
            e.tensor_scalar(head[:, 1, :], sr[:, :], 0.0, float(P - 1), ALU.min, ALU.mult)
            e.tensor_scalar(part[:, 1, :], sp[:, :], 0.0, float(P - 1), ALU.min, ALU.mult)
            link(e.tensor_scalar(part[:, 2, :], sp[:, :], 0.0, float(P), ALU.min, ALU.mult))
            pool_item(e, FIRST_TILES[0], -1)
            for j in range(GROUPS):
                e.tensor_scalar(lam_q[:, j, :], ramp, part[:, 0, j:j + 1], part[:, 1, j:j + 1], ALU.mult, ALU.add)
                e.tensor_scalar(lam_k[:, j, :], ramp_back, part[:, 0, j:j + 1], part[:, 2, j:j + 1], ALU.mult, ALU.add)
            for h in range(HEADS):
                last = e.tensor_scalar(mask[:, h, :], ramp_diff, head[:, 0, h:h + 1], head[:, 1, h:h + 1],
                                       ALU.mult, ALU.add)
                if h + 1 == HEADS // 2:
                    pool_item(e, FIRST_TILES[5], -1)
            last.then_inc(s_arg, 1)
            e.memset(state[:, 0, :, :], 0.0)
            for n in range(NBLK):
                bound = 0.0 if n % BPB == 0 else float(np.finfo(np.float32).max)
                e.memset(keep[:, 0, n:n + 1], -bound)
                e.memset(keep[:, 1, n:n + 1], bound)

            def rounded(c):
                w = raw(c)[0]
                e.wait_ge(s_inverse, 1 if c < KT else 2)
                link(e.tensor_scalar(w, w, beta[:, 4:5] if c < KT else beta[:, 5:6], MAGIC, ALU.mult, ALU.add))
                e.tensor_scalar(w, w, MAGIC + 1.0, MAGIC - 1.0, ALU.min, ALU.max).then_inc(s_clip_pool, 1)

            for c in range(POOL_TERNARY, KT):
                rounded(c)
            e.wait_ge(s_exp, 1)
            e.affine_select(out=mask[:, :, :], in_=mask[:, :, :], compare_op=ALU.is_ge, fill=0.0, base=0,
                            pattern=[[0, HEADS], [1, P]], channel_multiplier=-1).then_inc(s_mask, 1)

            def body(blk):
                for it in SEQUENCE_0 if isinstance(blk, int) else SEQUENCE:
                    if it[0] == "WP":
                        rounded(KT)
                    elif it[0] == "WC" and it[1] >= DVE_PIECES:
                        _, n, i = it
                        e.wait_ge(s_whi, 4 * n + i + 1)
                        hi_part, lo_part = piece_parts(n)
                        last = e.tensor_tensor(lo_part[:, i, :], slot(n)[:, i, :], hi_part[:, i, :], ALU.subtract)
                        if i == 3:
                            last.then_inc(cut(n)[0], 1)
                    else:
                        pool_item(e, it, blk)

            blocks(e, body)

        @block.scalar
        def _(e):
            e.sem_inc(ac["SILU"].sem, ac["SILU"].before)
            for dst, src in ((sr[:, :], s_row.partition_broadcast(P)), (sp[:, :], s_part)):
                e.dma_start(dst, src).then_inc(ld_tab, 16)

            def weight_sum(c):
                src, dst = raw(c)
                e.wait_ge(ld_qkv[c] if c < KT else ld_proj, 16)
                e.activation(dst, src, ACT.Abs, accum_out=beta[:, 12 + c:13 + c] if c < KT else beta[:, 1:2])\
                    .then_inc(s_abs, 1)

            def unmagic(c):
                src, dst = raw(c)
                e.wait_ge(*((s_clip, c + 1) if c < POOL_TERNARY else (s_clip_pool, c + 1 - POOL_TERNARY)))
                e.activation(dst, src, ACT.Copy, bias=-MAGIC).then_inc(s_tern, 1)

            for it in FIRST_TILES[:3]:
                scalar_item(e, it, -1)
            weight_sum(0)
            for it in FIRST_TILES[3:5]:
                scalar_item(e, it, -1)
            weight_sum(1)
            for it in FIRST_TILES[5:8]:
                scalar_item(e, it, -1)
            weight_sum(2)
            weight_sum(3)
            for it in FIRST_TILES[8:]:
                scalar_item(e, it, -1)
            e.wait_ge(s_arg, 1)
            e.activation(mask[:, :, :], mask[:, :, :], ACT.Exp).then_inc(s_exp, 1)
            e.activation(lam_q[:, :, :], lam_q[:, :, :], ACT.Exp)
            e.activation(lam_k[:, :, :], lam_k[:, :, :], ACT.Exp)
            e.activation(head[:, 2, :], head[:, 1, :], ACT.Exp, scale=-1.0)
            e.activation(part[:, 4, :], part[:, 0, :], ACT.Exp, scale=float(P))
            e.activation(part[:, 5, :], part[:, 2, :], ACT.Exp, scale=-1.0).then_inc(s_exp, 1)
            weight_sum(KT)
            unmagic(0)
            e.wait_ge(s_exp, 2)
            e.activation(lam_q[:, :, :], lam_q[:, :, :], ACT.Copy, scale=QL_SCALE)
            e.activation(lam_k[:, :, :], lam_k[:, :, :], ACT.Copy, scale=QKV_SCALE).then_inc(s_tab, 1)
            for c in range(1, KT):
                unmagic(c)
            e.wait_ge(s_mask, 1)
            e.activation(mask[:, :, :], mask[:, :, :], ACT.Copy, scale=SCORE_SCALE).then_inc(s_tab, 1)

            def body(blk):
                for it in SEQUENCE_0 if isinstance(blk, int) else SEQUENCE:
                    if it[0] == "WH":
                        _, n, i = it
                        e.wait_ge(s_scale, n + 1)
                        last = e.activation(piece_parts(n)[0][:, i, :], slot(n)[:, i, :], ACT.Copy, scale=ws[:, n:n + 1])
                        if n >= DVE_PIECES:
                            last = e.activation(slot(n)[:, i, :], slot(n)[:, i, :], ACT.Copy, scale=ws[:, n:n + 1])
                        last.then_inc(s_whi, 1)
                    elif it[0] == "WQ":
                        unmagic(KT)
                    scalar_item(e, it, blk)

            blocks(e, body)

        @block.tensor
        def _(e):
            e.sem_inc(pe["ZT"].sem, pe["ZT"].before)
            e.wait_ge(s_ident, 2)
            for it in FIRST_TILES:
                tensor_item(e, it, -1, FIRST_TILES)
            e.wait_ge(s_sum, 1)
            e.matmul(b_gate[:, 0:1], state1[:, :], beta[:, 0:1], start=True, stop=True).then_inc(s_ones, 1)
            e.wait_ge(s_abs, KT + 1)
            e.matmul(b_up[:, 0:1], state1[:, :], beta[:, 1:2], start=True, stop=True).then_inc(s_ones, 1)
            e.wait_ge(s_tern, KT)

            with e.Fori(0, NBLK) as blk:
                for it in SEQUENCE:
                    tensor_item(e, it, blk, SEQUENCE)

        @block.vector
        def _(e):
            done = [0]

            def link(ins):
                done[0] += 1
                ins.then_inc(s_pro, 1)
                e.wait_ge(s_pro, done[0])

            e.memset(diag[:, :], 0.0)
            link(e.memset(state1[:, :], 1.0))
            for h in range(HPG):
                r = slice(HD * h, HD * (h + 1))
                e.memset(diag[r, r], 1.0)
            for name in ("Q", "K", "KT", "KVM", "SM", "OUT", "SUM", "Z", "Y", "GT", "GL"):
                e.sem_inc(ve[name].sem, ve[name].before)
            vector_item(e, FIRST_TILES[0], -1)

            def power(a, b):
                link(e.tensor_scalar(am[:, a:b], am[:, a:b], LEAST, None, ALU.max))
                link(e.tensor_scalar(p2[:, a:b].bitcast(U32), am[:, a:b].bitcast(U32), 0x7F800000, None, ALU.bitwise_and))
                link(e.reciprocal(ip[:, a:b], p2[:, a:b]))

            e.wait_ge(ld_qn, 16)
            link(e.tensor_reduce(am[:, 12:13], qn_b[:, :], axis=AX.X, op=ALU.max, apply_absolute_value=True))
            power(12, 13)
            link(e.tensor_scalar(qn_b[:, :], qn_b[:, :], ip[:, 12:13], H_SCALE, ALU.mult, ALU.mult))
            for it in FIRST_TILES[1:8]:
                vector_item(e, it, -1)
            e.wait_ge(s_abs, KT)
            e.tensor_reduce(beta[:, 0:1], beta[:, 12:16], axis=AX.X, op=ALU.add).then_inc(s_sum, 1)
            for it in FIRST_TILES[8:]:
                vector_item(e, it, -1)
            e.wait_ge(s_ones, 1)
            link(e.tensor_scalar(beta[:, 2:3], b_gate[:, 0:1], 1.0 / (3 * D * D), 1e-5, ALU.mult, ALU.max))
            e.reciprocal(beta[:, 4:5], beta[:, 2:3]).then_inc(s_inverse, 1)
            e.wait_ge(s_inverse, 1)

            for c in range(POOL_TERNARY):
                w = raw(c)[0]
                link(e.tensor_scalar(w, w, beta[:, 4:5], MAGIC, ALU.mult, ALU.add))
                e.tensor_scalar(w, w, MAGIC + 1.0, MAGIC - 1.0, ALU.min, ALU.max).then_inc(s_clip, 1)
            e.wait_ge(s_ones, 2)
            link(e.tensor_scalar(beta[:, 3:4], b_up[:, 0:1], 1.0 / (D * D), 1e-5, ALU.mult, ALU.max))
            e.reciprocal(beta[:, 5:6], beta[:, 3:4]).then_inc(s_inverse, 1)
            e.sem_inc(ve["CHAIN"].sem, ve["CHAIN"].before - chain[0])
            link(e.tensor_scalar(beta[:, 6:7], beta[:, 2:3], p2[:, 12:13], 1.0 / H_SCALE, ALU.mult, ALU.mult))
            link(e.tensor_scalar(beta[:, 7:8], beta[:, 6:7], beta[:, 6:7], OUT_UNIT * HD ** -0.5, ALU.mult, ALU.mult))
            e.wait_ge(s_exp, 2)
            e.tensor_scalar(head[:, 3, :], head[:, 2, :], beta[:, 6:7], beta[:, 7:8], ALU.mult, ALU.mult)
            e.wait_ge(s_tab, 1)

            def weights(it):
                n = it[1]
                kind, q = PIECES[n]
                if it[0] == "WN":
                    e.wait_ge(ld_on, 32)
                    link(e.tensor_reduce(am[:, 13:14], op_b[:, :], axis=AX.X, op=ALU.max, apply_absolute_value=True))
                    power(13, 14)
                    link(e.tensor_tensor(op_b[:, :], op_b[:, :], on2_b[:, :], ALU.mult))
                    e.tensor_scalar(op_b[:, :], op_b[:, :], ip[:, 13:14], H_SCALE, ALU.mult, ALU.mult)
                    e.tensor_tensor(on2_b[:, :], on2_b[:, :], on2_b[:, :], ALU.mult)
                    link(e.tensor_scalar(beta[:, 8:9], beta[:, 3:4], p2[:, 13:14], 1.0 / H_SCALE, ALU.mult, ALU.mult))
                elif it[0] == "WA":
                    i = it[2]
                    e.wait_ge(ld_piece[n % 2], 16 * (n // 2 + 1))
                    if n and i == 0:
                        e.wait_ge(s_red, n)
                    last = e.tensor_reduce(pm4[:, i:i + 1], slot(n)[:, i, :], axis=AX.X, op=ALU.max,
                                           apply_absolute_value=True)
                    if i == 3:
                        link(last)
                        e.tensor_reduce(pm[:, n:n + 1], pm4[:, :], axis=AX.X, op=ALU.max).then_inc(s_red, 1)
                elif it[0] == "WB":
                    e.wait_ge(s_all[n % 2], 16 * (n // 2 + 1))
                    link(e.tensor_reduce(am[:, n:n + 1], max_row[n], axis=AX.X, op=ALU.max))
                    power(n, n + 1)
                    if kind == "gate":
                        e.tensor_scalar(sgate[:, q:q + 1], p2[:, n:n + 1], 2.0 ** -24, None, ALU.mult)
                        e.tensor_scalar(cu[:, q:q + 1], ip[:, n:n + 1], 2.0 ** -29, None, ALU.mult)
                    if kind == "down":
                        g, u = PIECES.index(("gate", q)), PIECES.index(("up", q))
                        link(e.tensor_scalar(cd[:, q:q + 1], p2[:, g:g + 1], p2[:, u:u + 1], None, ALU.mult))
                        e.tensor_scalar(cd[:, q:q + 1], cd[:, q:q + 1], p2[:, n:n + 1], 2.0 ** -9, ALU.mult, ALU.mult)
                    e.tensor_scalar(ws[:, n:n + 1], ip[:, n:n + 1], 2.0 ** 14, None, ALU.mult).then_inc(s_scale, 1)
                elif it[0] == "WC" and n < DVE_PIECES:
                    i = it[2]
                    e.wait_ge(s_whi, 4 * n + i + 1)
                    hi_part, lo_part = piece_parts(n)
                    last = e.scalar_tensor_tensor(out=lo_part[:, i, :], in0=slot(n)[:, i, :], scalar=ws[:, n:n + 1],
                                                  in1=hi_part[:, i, :], op0=ALU.mult, op1=ALU.subtract)
                    if i == 3:
                        last.then_inc(cut(n)[0], 1)

            def body(blk):
                chain[0] = 0
                if not isinstance(blk, int):
                    e.wait_ge(ve["S2"].sem, ve["S2"].at(blk, 0))
                    e.tensor_scalar(state[:, 0, :, :].rearrange("p j n -> p (j n)"),
                                    state[:, 0, :, :].rearrange("p j n -> p (j n)"),
                                    keep[:, 0, bass.ds(blk, 1)], keep[:, 1, bass.ds(blk, 1)], ALU.max, ALU.min)\
                        .then_inc(ve["KEEP"].sem, 1)
                    e.wait_ge(ve["KEEP"].sem, ve["KEEP"].at(blk, 0))
                for it in SEQUENCE_0 if isinstance(blk, int) else SEQUENCE:
                    if it[0][0] == "W":
                        weights(it)
                    else:
                        vector_item(e, it, blk)
                assert chain[0] == ve["CHAIN"].per

            blocks(e, body)


def kernel(L0_attn_x, L0_attn_qkv_w, L0_attn_qkv_norm_w, L0_attn_proj_w, L0_attn_proj_norm_w,
           L0_attn_norm_w, L0_attn_s, L0_ffn_w_gate, L0_ffn_w_up, L0_ffn_w_down):
    import concourse.bacc as bacc
    from concourse.bass_utils import run_bass_kernel_spmd

    def a(t):
        return np.asarray(t)

    hidden = lambda w: a(w).T.reshape(KT, P, NQ, HID // NQ).transpose(2, 1, 0, 3)
    arrays = {
        "x": a(L0_attn_x).reshape(TOK, D),
        "qkv_t": a(L0_attn_qkv_w).T.reshape(KT, P, 3 * D).transpose(1, 0, 2).reshape(P, KT * 3 * D),
        "proj_t": a(L0_attn_proj_w).T.reshape(KT, P, D).transpose(1, 0, 2).reshape(P, KT * D),
        "gate_t": hidden(L0_ffn_w_gate),
        "up_t": hidden(L0_ffn_w_up),
        "down_t": a(L0_ffn_w_down).T.reshape(NQ, HPQ, P, D).transpose(0, 2, 1, 3),
        "qn_w": a(L0_attn_qkv_norm_w), "on_w": a(L0_attn_norm_w), "pn_w": a(L0_attn_proj_norm_w),
        "s_row": a(L0_attn_s),
        "s_part": np.repeat(a(L0_attn_s).reshape(GROUPS, HPG).T, HD, axis=0),
    }
    arrays = {n: np.ascontiguousarray(t) for n, t in arrays.items()}
    nc = bacc.Bacc("TRN2", target_bir_lowering=False, num_devices=1, dynamic_dma_scratch_size=64)
    aps = [nc.dram_tensor(n, t.shape, mybir.dt.from_np(t.dtype), kind="ExternalInput").ap() for n, t in arrays.items()]
    out = nc.dram_tensor("out", (TOK, D), F32, kind="ExternalOutput").ap()
    spill = nc.dram_tensor("spill", (len(PIECES), P), F32).ap()
    build(nc, *aps, out, spill)
    r = run_bass_kernel_spmd(nc, [arrays], core_ids=[0])
    return r.results[0]["out"].reshape(BATCH, SEQ, D)
```
